# Optimizing a Trainium2 kernel written in Bass

```python
import numpy as np
import jax
import jax.numpy as jnp

def _softmax(x, axis=-1):
    return jax.nn.softmax(x, axis=axis)

def _gelu(x):
    return jax.nn.gelu(x, approximate=True)

def _silu(x):
    return jax.nn.silu(x)

def _sigmoid(x):
    return jax.nn.sigmoid(x)

def _layernorm(x, axis=-1, eps=1e-05):
    m = jnp.mean(x, axis=axis, keepdims=True)
    v = jnp.var(x, axis=axis, keepdims=True)
    return (x - m) / jnp.sqrt(v + eps)

def _scatter_add(tgt, idx, src, axis=0):
    return tgt.at[idx].add(src)

def _segment_sum(src, seg, n):
    return jax.ops.segment_sum(src, seg, n)
kernel_name = 'mk_decoder_postln_d2_seqx_r8_ac28d4'

def setup_inputs(seed: int=0):
    np.random.seed(seed)
    _w = jnp.asarray

    def _rec_inputs():
        import jax
        import jax.numpy as jnp
        _rk = jax.random.key(seed)
        x = 0.0002417 + 0.9998 * jax.random.normal(jax.random.fold_in(_rk, 1), (64, 128, 128), jnp.float32)
        _lenS = 128 - jax.random.randint(jax.random.fold_in(_rk, 7), (64,), 0, max(1, 128 // 4) + 1, jnp.int32)
        _lenS2 = 77 - jax.random.randint(jax.random.fold_in(_rk, 8), (64,), 0, max(1, 77 // 4) + 1, jnp.int32)
        _ctx_1024P = jax.random.normal(jax.random.fold_in(_rk, 11), (64, 16, 128), jnp.float32)
        _ctx_1024c = jax.random.dirichlet(jax.random.fold_in(_rk, 511), 0.3 * jnp.ones((16,), jnp.float32), (64, 77))
        _ctx_1024t = jnp.einsum('bsk,bkd->bsd', _ctx_1024c, _ctx_1024P)
        _ctx_1024t = _ctx_1024t * jax.lax.rsqrt(jnp.mean(jnp.square(_ctx_1024t)) + 1e-12) * 0.953939
        ctx_1024 = 7.22013e-05 + 1.00017 * (_ctx_1024t + 0.3 * jax.random.normal(jax.random.fold_in(_rk, 611), (64, 77, 128), jnp.float32))
        _validS = jnp.arange(128)[None, :] < _lenS[:, None]
        _validS2 = jnp.arange(77)[None, :] < _lenS2[:, None]
        _causal = jnp.tril(jnp.ones((128, 128), dtype=bool))
        mask_Bx1xSxS2_ik1 = jnp.where(jnp.broadcast_to(_validS2[:, None, None, :], (64, 1, 128, 77)), 1, 0).astype(jnp.int32)
        return (x, ctx_1024, mask_Bx1xSxS2_ik1)
    x, ctx_1024, mask_Bx1xSxS2_ik1 = _rec_inputs()

    def _L0_attn_setup():
        import jax, jax.numpy as jnp
        import numpy as np
        import math
        EMBED_DIM = 128
        NUM_HEADS = 16
        HEAD_DIM = EMBED_DIM // NUM_HEADS
        T, N = (128, 4)

        def _xavier(key, shape, fan_in, fan_out):
            bound = math.sqrt(6.0 / (fan_in + fan_out))
            return jax.random.uniform(key, shape, jnp.float32, -bound, bound)
        key = jax.random.key(seed)
        k1, k2, k3, k4 = jax.random.split(key, 4)
        x = jax.random.normal(k1, (T, N, EMBED_DIM), jnp.float32)
        q_weight = _xavier(k2, (EMBED_DIM, NUM_HEADS, HEAD_DIM), EMBED_DIM, EMBED_DIM)
        v_weight = _xavier(k3, (EMBED_DIM, NUM_HEADS, HEAD_DIM), EMBED_DIM, EMBED_DIM)
        out_w = _xavier(k4, (EMBED_DIM, EMBED_DIM), EMBED_DIM, EMBED_DIM)
        out_b = jnp.zeros((EMBED_DIM,), jnp.float32)
        return {'x': x, 'q_weight': q_weight, 'v_weight': v_weight, 'out_w': out_w, 'out_b': out_b}
    _L0_attn_all = _L0_attn_setup()
    _L0_attn_in = {k: v for k, v in _L0_attn_all.items() if k in ('q_weight', 'v_weight', 'out_w', 'out_b')}
    del _L0_attn_all

    def _L0_xattn_setup():
        import jax, jax.numpy as jnp
        import numpy as np
        EMBED = 128
        HEADS = 16
        HEAD_DIM = EMBED // HEADS
        B, S = (4, 256)
        key = jax.random.key(seed)
        ks = jax.random.split(key, 9)
        inp = {'values': jax.random.normal(ks[0], (B, S, EMBED), jnp.float32), 'keys': jax.random.normal(ks[1], (B, S, EMBED), jnp.float32), 'queries': jax.random.normal(ks[2], (B, S, EMBED), jnp.float32), 'mask': jax.random.randint(ks[3], (B, 1, S, S), 0, 2, jnp.int32), 'Wv': jax.random.normal(ks[4], (HEAD_DIM, HEAD_DIM), jnp.float32) / np.sqrt(HEAD_DIM), 'Wk': jax.random.normal(ks[5], (HEAD_DIM, HEAD_DIM), jnp.float32) / np.sqrt(HEAD_DIM), 'Wq': jax.random.normal(ks[6], (HEAD_DIM, HEAD_DIM), jnp.float32) / np.sqrt(HEAD_DIM), 'Wo': jax.random.normal(ks[7], (EMBED, EMBED), jnp.float32) / np.sqrt(EMBED), 'bo': jax.random.normal(ks[8], (EMBED,), jnp.float32) * 0.01}
        return inp
    _L0_xattn_all = _L0_xattn_setup()
    _L0_xattn_in = {k: v for k, v in _L0_xattn_all.items() if k in ('Wv', 'Wk', 'Wq', 'Wo', 'bo')}
    del _L0_xattn_all

    def _L0_ffn_setup():
        import jax, jax.numpy as jnp
        import numpy as np
        B, S, D = (2, 256, 128)
        E, K, H = (8, 4, 128)
        SH = 2 * H

        def _silu(x):
            return x * jax.nn.sigmoid(x)

        def _swiglu(x, w1, b1, w2, b2):
            return _silu(x @ w1 + b1) * (x @ w2 + b2)

        def _moe(x, gate_w, exp_w1, exp_w3, exp_w2, sh_w1, sh_w3, sh_w2):
            b, s, d = x.shape
            t = b * s
            xt = x.reshape(t, d)
            scores = jax.nn.softmax(xt @ gate_w.T, axis=-1)
            topv, topi = jax.lax.top_k(scores, K)
            topv = topv / jnp.sum(topv, axis=-1, keepdims=True)
            combine = jnp.zeros((t, E), xt.dtype).at[jnp.arange(t)[:, None], topi].set(topv)
            g = _silu(jnp.einsum('td,edh->eth', xt, exp_w1))
            u = jnp.einsum('td,edh->eth', xt, exp_w3)
            yexp = jnp.einsum('eth,ehd->etd', g * u, exp_w2)
            routed = jnp.einsum('te,etd->td', combine, yexp)
            shared = _silu(xt @ sh_w1) * (xt @ sh_w3) @ sh_w2
            return (routed + shared).reshape(b, s, d)
        key = jax.random.key(seed)
        ks = jax.random.split(key, 24)
        f = lambda k, shape: jax.random.normal(k, shape, dtype=jnp.float32) * 0.02
        return {'x': jax.random.normal(ks[0], (B, S, D), dtype=jnp.float32), 'lin0_w': f(ks[1], (D, D)), 'lin0_b': f(ks[2], (D,)), 'swi1_w1': f(ks[3], (D, D)), 'swi1_b1': f(ks[4], (D,)), 'swi1_w2': f(ks[5], (D, D)), 'swi1_b2': f(ks[6], (D,)), 'gate_w': f(ks[7], (E, D)), 'exp_w1': f(ks[8], (E, D, H)), 'exp_w3': f(ks[9], (E, D, H)), 'exp_w2': f(ks[10], (E, H, D)), 'sh_w1': f(ks[11], (D, SH)), 'sh_w3': f(ks[12], (D, SH)), 'sh_w2': f(ks[13], (SH, D)), 'lin1_w': f(ks[14], (D, D)), 'lin1_b': f(ks[15], (D,)), 'swi2_w1': f(ks[16], (D, D)), 'swi2_b1': f(ks[17], (D,)), 'swi2_w2': f(ks[18], (D, D)), 'swi2_b2': f(ks[19], (D,))}
    _L0_ffn_all = _L0_ffn_setup()
    _L0_ffn_in = {k: v for k, v in _L0_ffn_all.items() if k in ('lin0_w', 'lin0_b', 'swi1_w1', 'swi1_b1', 'swi1_w2', 'swi1_b2', 'gate_w', 'exp_w1', 'exp_w3', 'exp_w2', 'sh_w1', 'sh_w3', 'sh_w2', 'lin1_w', 'lin1_b', 'swi2_w1', 'swi2_b1', 'swi2_w2', 'swi2_b2')}
    del _L0_ffn_all

    def _L1_attn_setup():
        import jax, jax.numpy as jnp
        import numpy as np
        EMBED_DIM = 128
        NUM_HEADS = 16
        HEAD_DIM = EMBED_DIM // NUM_HEADS

        def _kernel_exp(x):
            return jnp.exp(x - jnp.max(x, axis=-1, keepdims=True))
        key = jax.random.key(seed)
        ks = jax.random.split(key, 9)
        s = 1.0 / np.sqrt(EMBED_DIM)
        inp = {'x': jax.random.normal(ks[0], (4, 1024, EMBED_DIM), dtype=jnp.float32)}
        for i, name in enumerate(['q', 'k', 'v', 'o']):
            inp[f'W{name}'] = jax.random.uniform(ks[1 + 2 * i], (EMBED_DIM, EMBED_DIM), jnp.float32, -s, s)
            inp[f'b{name}'] = jax.random.uniform(ks[2 + 2 * i], (EMBED_DIM,), jnp.float32, -s, s)
        return inp
    _L1_attn_all = _L1_attn_setup()
    _L1_attn_in = {k: v for k, v in _L1_attn_all.items() if k in ('Wq', 'bq', 'Wk', 'bk', 'Wv', 'bv', 'Wo', 'bo')}
    del _L1_attn_all

    def _L1_xattn_setup():
        import jax, jax.numpy as jnp
        import numpy as np
        D_MODEL = 128
        N_HEAD = 16
        D_K = 64
        D_V = 64
        B, S = (4, 256)
        key = jax.random.key(seed)
        ks = jax.random.split(key, 7)
        scale = 1.0 / np.sqrt(D_MODEL)
        return {'q': jax.random.normal(ks[0], (B, S, D_MODEL), jnp.float32), 'k': jax.random.normal(ks[1], (B, S, D_MODEL), jnp.float32), 'v': jax.random.normal(ks[2], (B, S, D_MODEL), jnp.float32), 'Wq': jax.random.normal(ks[3], (D_MODEL, N_HEAD * D_K), jnp.float32) * scale, 'Wk': jax.random.normal(ks[4], (D_MODEL, N_HEAD * D_K), jnp.float32) * scale, 'Wv': jax.random.normal(ks[5], (D_MODEL, N_HEAD * D_V), jnp.float32) * scale, 'Wo': jax.random.normal(ks[6], (N_HEAD * D_V, D_MODEL), jnp.float32) * scale}
    _L1_xattn_all = _L1_xattn_setup()
    _L1_xattn_in = {k: v for k, v in _L1_xattn_all.items() if k in ('Wq', 'Wk', 'Wv', 'Wo')}
    del _L1_xattn_all

    def _L1_ffn_setup():
        import jax, jax.numpy as jnp
        import numpy as np
        B, S, D, H, F = (4, 512, 128, 16, 512)
        CAP = 0.125
        ROPE_BASE = 10000.0

        def rmsnorm(x, g):
            return x * jax.lax.rsqrt(jnp.mean(x * x, -1, keepdims=True) + 1e-06) * g

        def rope(t, pos):
            hd = t.shape[-1]
            inv = 1.0 / ROPE_BASE ** (jnp.arange(0, hd, 2, dtype=jnp.float32) / hd)
            f = pos[:, None, :, None].astype(jnp.float32) * inv
            emb = jnp.concatenate([f, f], axis=-1)
            cos, sin = (jnp.cos(emb), jnp.sin(emb))
            rot = jnp.concatenate([-t[..., hd // 2:], t[..., :hd // 2]], axis=-1)
            return t * cos + rot * sin
        key = jax.random.key(seed)
        ks = jax.random.split(key, 9)
        scale = 0.02
        x = jax.random.normal(ks[0], (B, S, D), jnp.float32)
        causal = jnp.where(jnp.tril(jnp.ones((S, S), bool)), 0.0, -1000000000.0).astype(jnp.float32)
        attention_mask = jnp.broadcast_to(causal[None, None], (B, 1, S, S))
        position_ids = jnp.broadcast_to(jnp.arange(S, dtype=jnp.int32), (B, S))
        return {'x': x, 'attention_mask': attention_mask, 'position_ids': position_ids, 'router_w': jax.random.normal(ks[1], (D, 1), jnp.float32) * scale, 'router_b': jnp.zeros((1,), jnp.float32), 'wq': jax.random.normal(ks[2], (D, D), jnp.float32) * scale, 'wk': jax.random.normal(ks[3], (D, D), jnp.float32) * scale, 'wv': jax.random.normal(ks[4], (D, D), jnp.float32) * scale, 'wo': jax.random.normal(ks[5], (D, D), jnp.float32) * scale, 'w1': jax.random.normal(ks[6], (D, F), jnp.float32) * scale, 'w2': jax.random.normal(ks[7], (F, D), jnp.float32) * scale, 'ln1': jnp.ones((D,), jnp.float32), 'ln2': jnp.ones((D,), jnp.float32)}
    _L1_ffn_all = _L1_ffn_setup()
    _L1_ffn_in = {k: v for k, v in _L1_ffn_all.items() if k in ('attention_mask', 'position_ids', 'router_w', 'router_b', 'wq', 'wk', 'wv', 'wo', 'w1', 'w2', 'ln1', 'ln2')}
    del _L1_ffn_all
    return {'x': x, 'ctx_1024': ctx_1024, 'mask_Bx1xSxS2_ik1': mask_Bx1xSxS2_ik1, 'L0_attn_q_weight': _L0_attn_in['q_weight'], 'L0_attn_v_weight': _L0_attn_in['v_weight'], 'L0_attn_out_w': _L0_attn_in['out_w'], 'L0_attn_out_b': _L0_attn_in['out_b'], 'L0_xattn_Wv': _L0_xattn_in['Wv'], 'L0_xattn_Wk': _L0_xattn_in['Wk'], 'L0_xattn_Wq': _L0_xattn_in['Wq'], 'L0_xattn_Wo': _L0_xattn_in['Wo'], 'L0_xattn_bo': _L0_xattn_in['bo'], 'L0_ffn_lin0_w': _L0_ffn_in['lin0_w'], 'L0_ffn_lin0_b': _L0_ffn_in['lin0_b'], 'L0_ffn_swi1_w1': _L0_ffn_in['swi1_w1'], 'L0_ffn_swi1_b1': _L0_ffn_in['swi1_b1'], 'L0_ffn_swi1_w2': _L0_ffn_in['swi1_w2'], 'L0_ffn_swi1_b2': _L0_ffn_in['swi1_b2'], 'L0_ffn_gate_w': _L0_ffn_in['gate_w'], 'L0_ffn_exp_w1': _L0_ffn_in['exp_w1'], 'L0_ffn_exp_w3': _L0_ffn_in['exp_w3'], 'L0_ffn_exp_w2': _L0_ffn_in['exp_w2'], 'L0_ffn_sh_w1': _L0_ffn_in['sh_w1'], 'L0_ffn_sh_w3': _L0_ffn_in['sh_w3'], 'L0_ffn_sh_w2': _L0_ffn_in['sh_w2'], 'L0_ffn_lin1_w': _L0_ffn_in['lin1_w'], 'L0_ffn_lin1_b': _L0_ffn_in['lin1_b'], 'L0_ffn_swi2_w1': _L0_ffn_in['swi2_w1'], 'L0_ffn_swi2_b1': _L0_ffn_in['swi2_b1'], 'L0_ffn_swi2_w2': _L0_ffn_in['swi2_w2'], 'L0_ffn_swi2_b2': _L0_ffn_in['swi2_b2'], 'L1_attn_Wq': _L1_attn_in['Wq'], 'L1_attn_bq': _L1_attn_in['bq'], 'L1_attn_Wk': _L1_attn_in['Wk'], 'L1_attn_bk': _L1_attn_in['bk'], 'L1_attn_Wv': _L1_attn_in['Wv'], 'L1_attn_bv': _L1_attn_in['bv'], 'L1_attn_Wo': _L1_attn_in['Wo'], 'L1_attn_bo': _L1_attn_in['bo'], 'L1_xattn_Wq': _L1_xattn_in['Wq'], 'L1_xattn_Wk': _L1_xattn_in['Wk'], 'L1_xattn_Wv': _L1_xattn_in['Wv'], 'L1_xattn_Wo': _L1_xattn_in['Wo'], 'L1_ffn_attention_mask': _L1_ffn_in['attention_mask'], 'L1_ffn_position_ids': _L1_ffn_in['position_ids'], 'L1_ffn_router_w': _L1_ffn_in['router_w'], 'L1_ffn_router_b': _L1_ffn_in['router_b'], 'L1_ffn_wq': _L1_ffn_in['wq'], 'L1_ffn_wk': _L1_ffn_in['wk'], 'L1_ffn_wv': _L1_ffn_in['wv'], 'L1_ffn_wo': _L1_ffn_in['wo'], 'L1_ffn_w1': _L1_ffn_in['w1'], 'L1_ffn_w2': _L1_ffn_in['w2'], 'L1_ffn_ln1': _L1_ffn_in['ln1'], 'L1_ffn_ln2': _L1_ffn_in['ln2']}

def reference(x, ctx_1024, mask_Bx1xSxS2_ik1, L0_attn_q_weight, L0_attn_v_weight, L0_attn_out_w, L0_attn_out_b, L0_xattn_Wv, L0_xattn_Wk, L0_xattn_Wq, L0_xattn_Wo, L0_xattn_bo, L0_ffn_lin0_w, L0_ffn_lin0_b, L0_ffn_swi1_w1, L0_ffn_swi1_b1, L0_ffn_swi1_w2, L0_ffn_swi1_b2, L0_ffn_gate_w, L0_ffn_exp_w1, L0_ffn_exp_w3, L0_ffn_exp_w2, L0_ffn_sh_w1, L0_ffn_sh_w3, L0_ffn_sh_w2, L0_ffn_lin1_w, L0_ffn_lin1_b, L0_ffn_swi2_w1, L0_ffn_swi2_b1, L0_ffn_swi2_w2, L0_ffn_swi2_b2, L1_attn_Wq, L1_attn_bq, L1_attn_Wk, L1_attn_bk, L1_attn_Wv, L1_attn_bv, L1_attn_Wo, L1_attn_bo, L1_xattn_Wq, L1_xattn_Wk, L1_xattn_Wv, L1_xattn_Wo, L1_ffn_attention_mask, L1_ffn_position_ids, L1_ffn_router_w, L1_ffn_router_b, L1_ffn_wq, L1_ffn_wk, L1_ffn_wv, L1_ffn_wo, L1_ffn_w1, L1_ffn_w2, L1_ffn_ln1, L1_ffn_ln2):
    import jax
    import jax.numpy as jnp

    def _L0_attn_ref(x, q_weight, v_weight, out_w, out_b):
        import jax, jax.numpy as jnp
        import numpy as np
        import math
        EMBED_DIM = 128
        NUM_HEADS = 16
        HEAD_DIM = EMBED_DIM // NUM_HEADS
        T, N = (128, 4)

        def _xavier(key, shape, fan_in, fan_out):
            bound = math.sqrt(6.0 / (fan_in + fan_out))
            return jax.random.uniform(key, shape, jnp.float32, -bound, bound)
        head_dim = q_weight.shape[-1]
        scale = 1.0 / math.sqrt(head_dim)
        q = jnp.einsum('tbm,mhd->tbhd', x, q_weight)
        k = jnp.einsum('tbm,mhd->tbhd', x, q_weight)
        qq = jnp.sum(q * q, axis=-1)
        kk = jnp.sum(k * k, axis=-1)
        qk = jnp.einsum('tbhd,sbhd->tsbh', q, k)
        squared_dist = qq[:, None] + kk[None, :] - 2.0 * qk
        attn_logits = -squared_dist * scale
        attn_weights = jax.nn.softmax(attn_logits, axis=1)
        A = jnp.einsum('mhd,nhd->hmn', q_weight, q_weight) * scale
        XA = jnp.einsum('tbm,hmn->tbhn', x, A)
        PXA = jnp.einsum('tsbh,sbhm->tbhm', attn_weights, XA)
        PXAV = jnp.einsum('tbhm,mhd->tbhd', PXA, v_weight).reshape(x.shape[0], x.shape[1], -1)
        return PXAV @ out_w.T + out_b

    def _L0_xattn_ref(values, keys, queries, mask, Wv, Wk, Wq, Wo, bo):
        import jax, jax.numpy as jnp
        import numpy as np
        EMBED = 128
        HEADS = 16
        HEAD_DIM = EMBED // HEADS
        B, S = (4, 256)
        N, q_len = (queries.shape[0], queries.shape[1])
        v_len, k_len = (values.shape[1], keys.shape[1])
        v = values.reshape(N, v_len, HEADS, HEAD_DIM)
        k = keys.reshape(N, k_len, HEADS, HEAD_DIM)
        q = queries.reshape(N, q_len, HEADS, HEAD_DIM)
        v = jnp.einsum('nlhd,ed->nlhe', v, Wv)
        k = jnp.einsum('nlhd,ed->nlhe', k, Wk)
        q = jnp.einsum('nlhd,ed->nlhe', q, Wq)
        energy = jnp.einsum('nqhd,nkhd->nhqk', q, k)
        energy = jnp.where(mask == 0, jnp.float32(-1e+20), energy)
        attention = jax.nn.softmax(energy / np.sqrt(EMBED).astype(np.float32), axis=3)
        out = jnp.einsum('nhql,nlhd->nqhd', attention, v).reshape(N, q_len, EMBED)
        return out @ Wo.T + bo

    def _L0_ffn_ref(x, lin0_w, lin0_b, swi1_w1, swi1_b1, swi1_w2, swi1_b2, gate_w, exp_w1, exp_w3, exp_w2, sh_w1, sh_w3, sh_w2, lin1_w, lin1_b, swi2_w1, swi2_b1, swi2_w2, swi2_b2):
        import jax, jax.numpy as jnp
        import numpy as np
        B, S, D = (2, 256, 128)
        E, K, H = (8, 4, 128)
        SH = 2 * H

        def _silu(x):
            return x * jax.nn.sigmoid(x)

        def _swiglu(x, w1, b1, w2, b2):
            return _silu(x @ w1 + b1) * (x @ w2 + b2)

        def _moe(x, gate_w, exp_w1, exp_w3, exp_w2, sh_w1, sh_w3, sh_w2):
            b, s, d = x.shape
            t = b * s
            xt = x.reshape(t, d)
            scores = jax.nn.softmax(xt @ gate_w.T, axis=-1)
            topv, topi = jax.lax.top_k(scores, K)
            topv = topv / jnp.sum(topv, axis=-1, keepdims=True)
            combine = jnp.zeros((t, E), xt.dtype).at[jnp.arange(t)[:, None], topi].set(topv)
            g = _silu(jnp.einsum('td,edh->eth', xt, exp_w1))
            u = jnp.einsum('td,edh->eth', xt, exp_w3)
            yexp = jnp.einsum('eth,ehd->etd', g * u, exp_w2)
            routed = jnp.einsum('te,etd->td', combine, yexp)
            shared = _silu(xt @ sh_w1) * (xt @ sh_w3) @ sh_w2
            return (routed + shared).reshape(b, s, d)
        h = x @ lin0_w + lin0_b
        h = _swiglu(h, swi1_w1, swi1_b1, swi1_w2, swi1_b2)
        h = _moe(h, gate_w, exp_w1, exp_w3, exp_w2, sh_w1, sh_w3, sh_w2)
        h = h @ lin1_w + lin1_b
        h = _swiglu(h, swi2_w1, swi2_b1, swi2_w2, swi2_b2)
        return h

    def _L1_attn_ref(x, Wq, bq, Wk, bk, Wv, bv, Wo, bo):
        import jax, jax.numpy as jnp
        import numpy as np
        EMBED_DIM = 128
        NUM_HEADS = 16
        HEAD_DIM = EMBED_DIM // NUM_HEADS

        def _kernel_exp(x):
            return jnp.exp(x - jnp.max(x, axis=-1, keepdims=True))
        b, s, e = x.shape

        def proj(W, bias):
            return (x @ W.T + bias).reshape(b, s, NUM_HEADS, HEAD_DIM).transpose(0, 2, 1, 3)
        q = proj(Wq, bq)
        k = proj(Wk, bk)
        v = proj(Wv, bv)
        q_kern = _kernel_exp(q)
        k_kern = _kernel_exp(k)
        kv = jnp.einsum('bhsd,bhse->bhde', k_kern, v)
        k_sum = jnp.sum(k_kern, axis=2)
        denom = jnp.einsum('bhqd,bhd->bhq', q_kern, k_sum) + 1e-06
        y = jnp.einsum('bhqd,bhde->bhqe', q_kern, kv) / denom[..., None]
        y = y.transpose(0, 2, 1, 3).reshape(b, s, e)
        return y @ Wo.T + bo

    def _L1_xattn_ref(q, k, v, Wq, Wk, Wv, Wo):
        import jax, jax.numpy as jnp
        import numpy as np
        D_MODEL = 128
        N_HEAD = 16
        D_K = 64
        D_V = 64
        B, S = (4, 256)
        B_, Sq, _ = q.shape
        Sk = k.shape[1]
        qh = (q @ Wq).reshape(B_, Sq, N_HEAD, D_K).transpose(0, 2, 1, 3)
        kh = (k @ Wk).reshape(B_, Sk, N_HEAD, D_K).transpose(0, 2, 1, 3)
        vh = (v @ Wv).reshape(B_, Sk, N_HEAD, D_V).transpose(0, 2, 1, 3)
        scores = jnp.einsum('bhqd,bhkd->bhqk', qh, kh) / jnp.sqrt(jnp.float32(D_K))
        attn = jax.nn.softmax(scores, axis=-1)
        ctx = jnp.einsum('bhqk,bhkd->bhqd', attn, vh)
        ctx = ctx.transpose(0, 2, 1, 3).reshape(B_, Sq, N_HEAD * D_V)
        return ctx @ Wo

    def _L1_ffn_ref(x, attention_mask, position_ids, router_w, router_b, wq, wk, wv, wo, w1, w2, ln1, ln2):
        import jax, jax.numpy as jnp
        import numpy as np
        B, S, D, H, F = (4, 512, 128, 16, 512)
        CAP = 0.125
        ROPE_BASE = 10000.0

        def rmsnorm(x, g):
            return x * jax.lax.rsqrt(jnp.mean(x * x, -1, keepdims=True) + 1e-06) * g

        def rope(t, pos):
            hd = t.shape[-1]
            inv = 1.0 / ROPE_BASE ** (jnp.arange(0, hd, 2, dtype=jnp.float32) / hd)
            f = pos[:, None, :, None].astype(jnp.float32) * inv
            emb = jnp.concatenate([f, f], axis=-1)
            cos, sin = (jnp.cos(emb), jnp.sin(emb))
            rot = jnp.concatenate([-t[..., hd // 2:], t[..., :hd // 2]], axis=-1)
            return t * cos + rot * sin
        b, s, d = x.shape
        hd = d // H
        weights = (x @ router_w)[..., 0] + router_b[0]
        k = int(CAP * s)
        topv, topi = jax.lax.top_k(weights, k)
        thr = topv[:, -1]
        sel_mask = (weights > thr[:, None]).astype(x.dtype)
        kc = k - 1
        sel_idx = jnp.sort(topi[:, :kc], axis=1)
        bidx = jnp.arange(b)[:, None]
        x_sel = x[bidx, sel_idx]
        pos_sel = position_ids[bidx, sel_idx]
        w_sel = weights[bidx, sel_idx]
        m = attention_mask[:, 0]
        m_sel = m[bidx[:, :, None], sel_idx[:, :, None], sel_idx[:, None, :]]
        hn = rmsnorm(x_sel, ln1)

        def heads(t):
            return t.reshape(b, kc, H, hd).transpose(0, 2, 1, 3)
        q = rope(heads(hn @ wq), pos_sel)
        kk = rope(heads(hn @ wk), pos_sel)
        v = heads(hn @ wv)
        sc = jnp.einsum('bhqd,bhkd->bhqk', q, kk) / np.sqrt(hd).astype(np.float32)
        sc = sc + m_sel[:, None]
        a = jax.nn.softmax(sc, axis=-1)
        o = jnp.einsum('bhqk,bhkd->bhqd', a, v).transpose(0, 2, 1, 3).reshape(b, kc, d) @ wo
        x1 = x_sel + o
        x2 = x1 + jax.nn.gelu(rmsnorm(x1, ln2) @ w1) @ w2
        proc = x2 * w_sel[..., None]
        out = jnp.zeros_like(x).at[bidx, sel_idx].set(proc)
        return out + x * (1.0 - sel_mask)[..., None]
    x = _layernorm(x + _L0_attn_ref(x, L0_attn_q_weight, L0_attn_v_weight, L0_attn_out_w, L0_attn_out_b), axis=-1)
    x = _layernorm(x + _L0_xattn_ref(ctx_1024, ctx_1024, x, mask_Bx1xSxS2_ik1, L0_xattn_Wv, L0_xattn_Wk, L0_xattn_Wq, L0_xattn_Wo, L0_xattn_bo), axis=-1)
    x = _layernorm(x + _L0_ffn_ref(x, L0_ffn_lin0_w, L0_ffn_lin0_b, L0_ffn_swi1_w1, L0_ffn_swi1_b1, L0_ffn_swi1_w2, L0_ffn_swi1_b2, L0_ffn_gate_w, L0_ffn_exp_w1, L0_ffn_exp_w3, L0_ffn_exp_w2, L0_ffn_sh_w1, L0_ffn_sh_w3, L0_ffn_sh_w2, L0_ffn_lin1_w, L0_ffn_lin1_b, L0_ffn_swi2_w1, L0_ffn_swi2_b1, L0_ffn_swi2_w2, L0_ffn_swi2_b2), axis=-1)
    x = _layernorm(x + _L1_attn_ref(x, L1_attn_Wq, L1_attn_bq, L1_attn_Wk, L1_attn_bk, L1_attn_Wv, L1_attn_bv, L1_attn_Wo, L1_attn_bo), axis=-1)
    x = _layernorm(x + _L1_xattn_ref(x, ctx_1024, ctx_1024, L1_xattn_Wq, L1_xattn_Wk, L1_xattn_Wv, L1_xattn_Wo), axis=-1)
    x = _layernorm(x + _L1_ffn_ref(x, L1_ffn_attention_mask, L1_ffn_position_ids, L1_ffn_router_w, L1_ffn_router_b, L1_ffn_wq, L1_ffn_wk, L1_ffn_wv, L1_ffn_wo, L1_ffn_w1, L1_ffn_w2, L1_ffn_ln1, L1_ffn_ln2), axis=-1)
    return x

_drawn_inputs = setup_inputs


def setup_inputs(seed=0):
    import zlib

    import numpy as np

    out = dict(_drawn_inputs(seed))
    spreads = {'L0_attn_out_b': (0.0, 0.1), 'L1_ffn_ln1': (1.0, 0.6), 'L1_ffn_ln2': (1.0, 0.6)}
    factors = {'L0_xattn_bo': 8.0,
     'L0_ffn_lin0_w': 8.0,
     'L0_ffn_lin0_b': 8.0,
     'L0_ffn_swi1_w1': 8.0,
     'L0_ffn_swi1_b1': 8.0,
     'L0_ffn_swi1_w2': 8.0,
     'L0_ffn_swi1_b2': 8.0,
     'L0_ffn_gate_w': 8.0,
     'L0_ffn_exp_w1': 8.0,
     'L0_ffn_exp_w3': 8.0,
     'L0_ffn_exp_w2': 8.0,
     'L0_ffn_sh_w1': 8.0,
     'L0_ffn_sh_w3': 8.0,
     'L0_ffn_sh_w2': 8.0,
     'L0_ffn_lin1_w': 8.0,
     'L0_ffn_lin1_b': 64.0,
     'L0_ffn_swi2_w1': 8.0,
     'L0_ffn_swi2_b1': 64.0,
     'L0_ffn_swi2_w2': 8.0,
     'L0_ffn_swi2_b2': 64.0,
     'L1_attn_Wq': 8.0,
     'L1_attn_bq': 8.0,
     'L1_attn_Wk': 8.0,
     'L1_attn_bk': 8.0,
     'L1_attn_bv': 2.862,
     'L1_ffn_router_w': 8.0,
     'L1_ffn_wq': 8.0,
     'L1_ffn_wk': 8.0,
     'L1_ffn_wv': 8.0,
     'L1_ffn_wo': 8.0,
     'L1_ffn_w1': 8.0,
     'L1_ffn_w2': 8.0}
    for name, (base, spread) in spreads.items():
        noise = np.random.default_rng([zlib.crc32(name.encode()), seed]).standard_normal(out[name].shape)
        drawn = base * np.exp(spread * noise) if base else spread * noise
        out[name] = jnp.asarray(drawn.astype(out[name].dtype))
    for name, factor in factors.items():
        out[name] = (out[name] * factor).astype(out[name].dtype)
    return out
```

```python
from contextlib import ExitStack

import numpy as np

import concourse.bass as bass
import concourse.mybir as mybir
from concourse.alu_op_type import AluOpType as ALU

F32 = mybir.dt.float32
BF16 = mybir.dt.bfloat16
I32 = mybir.dt.int32
U32 = mybir.dt.uint32
ACT = mybir.ActivationFunctionType
AX = mybir.AxisListType

B, S, D = 64, 128, 128
SC = 77
H, HD = 16, 8
DK = 64
E, TOPK = 8, 4
EPS = 1e-5


class Frame:

    def __init__(self, nc, ctx, tag):
        self.nc, self.ctx, self.tag = nc, ctx, tag

    def sb(self, name, shape, dt=F32):
        return self.ctx.enter_context(self.nc.sbuf_tensor(f"{self.tag}_{name}", shape, dt))

    def ps(self, name, shape, dt=F32):
        return self.ctx.enter_context(self.nc.psum_tensor(f"{self.tag}_{name}", shape, dt))

    def sems(self, *names):
        made = [self.nc.alloc_semaphore(name=f"{self.tag}_{n}") for n in names]
        self.ctx.callback(self.clear, made)
        return made

    def clear(self, made):
        self.nc.clear_and_free_semaphores(made)
        self.nc.all_engine_barrier()

    def block(self):
        return self.ctx.enter_context(self.nc.Block())


def done(eng, sem, n, per=1):
    if isinstance(n, int) and n < 0:
        return
    eng.wait_ge(sem, n * per + per)


class Steps:

    def __init__(self, count, ahead, behind, first, unroll=2):
        self.count, self.ahead, self.behind, self.unroll = count, ahead, behind, unroll
        self.first = -(-max(first, behind) // unroll) * unroll

    def has(self, n):
        return not isinstance(n, int) or 0 <= n < self.count

    def run(self, eng, body):
        u = self.unroll
        start = self.first
        turns = (self.count - self.ahead - start) // u
        for n in range(-self.ahead, start):
            body(n, n % u)
        with eng.Fori(0, turns) as i:
            for k in range(u):
                body(i * u + start + k, k)
        for n in range(start + u * turns, self.count + self.behind):
            body(n, n % u)



def load(nc, items, tag="load"):
    with ExitStack() as ctx:
        f = Frame(nc, ctx, tag)
        landed, landed2 = f.sems("landed", "landed2")
        block = f.block()
        half = (len(items) + 1) // 2

        @block.sync
        def _(sp):
            for dst, src in items[:half]:
                sp.dma_start(dst, src).then_inc(landed, 16)
            sp.wait_ge(landed, 16 * half)

        @block.scalar
        def _(act):
            for dst, src in items[half:]:
                act.dma_start(dst, src).then_inc(landed2, 16)
            act.wait_ge(landed2, 16 * (len(items) - half))


def row_stats(nc, st):
    with ExitStack() as ctx:
        f = Frame(nc, ctx, "rows")
        (stats,) = f.sems("stats")
        block = f.block()

        @block.vector
        def _(dve):
            PART = 16
            with dve.Fori(0, B // PART) as i:
                for k in range(PART):
                    nc.vector.bn_stats(st.STATS[:, i * PART + k, :], st.X[:, i * PART + k, :]).then_inc(stats, 1)
            dve.wait_ge(stats, B)


def norm_rows(nc, st, tag):
    with ExitStack() as ctx:
        f = Frame(nc, ctx, tag)
        d, v, w, std = (f.sb(n, [S, B]) for n in ("diff", "var", "work", "std"))
        vec, var_ready, std_ready = f.sems("vec", "var_ready", "std_ready")
        block = f.block()
        me, cve = st.STATS[:, :, 1], st.STATS[:, :, 2]
        mo, cvo = st.STATS[:, :, 4], st.STATS[:, :, 5]

        @block.vector
        def _(dve):
            nc.vector.tensor_tensor(st.MEAN[:], me, mo, ALU.add).then_inc(vec, 1)
            nc.vector.tensor_tensor(d[:], me, mo, ALU.subtract).then_inc(vec, 1)
            nc.vector.tensor_tensor(v[:], cve, cvo, ALU.add).then_inc(vec, 1)
            dve.wait_ge(vec, 3)
            nc.vector.tensor_tensor(w[:], d[:], d[:], ALU.mult).then_inc(vec, 1)
            nc.vector.tensor_scalar(st.MEAN[:], st.MEAN[:], 0.5, None, ALU.mult).then_inc(vec, 1)
            dve.wait_ge(vec, 4)
            nc.vector.tensor_scalar(d[:], w[:], D / 4, None, ALU.mult).then_inc(vec, 1)
            dve.wait_ge(vec, 6)
            nc.vector.tensor_tensor(w[:], v[:], d[:], ALU.add).then_inc(vec, 1)
            dve.wait_ge(vec, 7)
            nc.vector.tensor_scalar(v[:], w[:], 1.0 / D, EPS, ALU.mult, ALU.add).then_inc(var_ready, 1)
            dve.wait_ge(std_ready, 1)
            nc.vector.reciprocal(st.RSTD[:], std[:]).then_inc(vec, 1)
            dve.wait_ge(vec, 8)
            nc.vector.scalar_tensor_tensor(out=st.SHIFT[:], in0=st.MEAN[:], scalar=-1.0, in1=st.RSTD[:],
                                           op0=ALU.mult, op1=ALU.mult)

        @block.scalar
        def _(act):
            act.wait_ge(var_ready, 1)
            nc.scalar.activation(std[:], v[:], ACT.Sqrt).then_inc(std_ready, 1)



def phase_a(nc, st, x, sums, later):
    G, HG, T = 4, 4, B
    N = S // 2
    plan = Steps(N, 2, 2, 3)
    PARTS = 8
    FIRST = 8
    with ExitStack() as ctx:
        f = Frame(nc, ctx, "a")
        x_t = f.sb("x", [128, 2, D])
        xa = f.sb("xa", [128, N, D])
        xT = f.sb("xT", [D, 2, 128])
        ka = f.sb("ka", [128, 2, G, 128])
        y = f.sb("y", [128, 2, G, 128])
        qb = f.sb("qb", [128, 2, G, HG, 128])
        vbd = f.sb("vbd", [128, 2, H, 2, 9])
        p = f.sb("p", [128, 2, 2, 512])
        rec = f.sb("rec", [128, 8, 2])
        ob = f.sb("ob", [128, D])
        o = f.sb("o", [128, 2, 8, HD])
        oT = f.sb("oT", [128, 128])
        val = f.sb("val", [128, 128])
        cbd = f.sb("cbd", [128, 128])
        ps_x = f.ps("ps_x", [128, 512])
        ps_q = f.ps("ps_q", [128, G, 128])
        ps_v = f.ps("ps_v", [128, 512])
        ps_s = f.ps("ps_s", [128, 2, 512])
        ps_av = f.ps("ps_av", [128, 512])
        ps_oT = f.ps("ps_oT", [128, 512])
        ps_out = f.ps("ps_out", [128, 512])
        av = ps_av[:, 0:8 * 18].rearrange("p (q j e) -> p q j e", j=2, e=9)
        (cst, wv_ps, wv_sb, first_in, landed, x_sb, xT_ps, xT_sb, q_ps, v_ps, ka_sb, y_sb, qb_sb, ql_sb, v_sb, s_ps,
         p_sb, av_ps, rec_sb, o_sb, oT_ps, oT_sb, out_ps, ob_sb, r_sb, stored,
         back_in, later_in) = f.sems(
            "cst", "wv_ps", "wv_sb", "first_in", "landed", "x_sb", "xT_ps", "xT_sb", "q_ps", "v_ps", "ka_sb", "y_sb",
            "qb_sb", "ql_sb", "v_sb", "s_ps", "p_sb", "av_ps", "rec_sb", "o_sb", "oT_ps", "oT_sb", "out_ps",
            "ob_sb", "r_sb", "stored", "back_in", "later_in")
        block = f.block()
        x_h = x.rearrange("t (n j) d -> j t n d", j=2)
        r_h = sums.rearrange("t (n j) d -> j t n d", j=2)
        back = sums.rearrange("t p d -> p t d")
        c2 = 2.0 / float(np.sqrt(HD))

        @block.sync
        def _(sp):
            for part, sem in ((slice(0, FIRST), first_in), (slice(FIRST, N // 2), landed), (slice(N // 2, N), landed)):
                for j in range(2):
                    sp.dma_start(xa[64 * j:64 * j + 64, part, :], x_h[j][:, part, :]).then_inc(sem, 16)
            for dst, src in later:
                sp.dma_start(dst, src).then_inc(later_in, 16)
            for c in range(PARTS):
                part = slice(c * N // PARTS, (c + 1) * N // PARTS)
                sp.wait_ge(r_sb, (c + 1) * N // PARTS)
                for j in range(2):
                    sp.dma_start(r_h[j][:, part, :], xa[64 * j:64 * j + 64, part, :]).then_inc(stored, 16)
                sp.wait_ge(stored, 32 * (c + 1))
                rows = slice(c * S // PARTS, (c + 1) * S // PARTS)
                sp.dma_start(st.X[rows], back[rows]).then_inc(back_in, 16)
            sp.wait_ge(back_in, 16 * PARTS)
            sp.wait_ge(later_in, 16 * len(later))

        @block.gpsimd
        def _(pool):
            pool.wait_ge(first_in, 32)

            def masked(n, s):
                done(pool, y_sb, n)
                done(pool, s_ps, n - 2)
                nc.gpsimd.tensor_tensor(qb[:, s, :, HG - 1, :], y[:, s],
                                        st.w["a_mask"][:, HG - 1:HG].unsqueeze(2).to_broadcast([128, G, 128]),
                                        ALU.mult).then_inc(ql_sb, 1)

            def step(n, s):
                if isinstance(n, int) and n == plan.first - 1:
                    pool.wait_ge(landed, 64)
                if plan.has(n + 2):
                    done(pool, xT_ps, n)
                    nc.gpsimd.tensor_copy(x_t[:, s, :], xa[:, n + 2, :]).then_inc(x_sb, 1)
                if plan.has(n + 1):
                    masked(n + 1, 1 - s)
            plan.run(pool, step)

        @block.scalar
        def _(act):
            act.wait_ge(cst, 6)
            act.wait_ge(wv_ps, 2)
            nc.scalar.activation(val[:], ps_out[:, 0:128], ACT.Copy, scale=0.5 * c2).then_inc(wv_sb, 1)

            def x_rows(n, s):
                done(act, xT_ps, n)
                done(act, v_ps, n - 2)
                nc.scalar.activation(xT[:, s, :], ps_x[:, 0:128], ACT.Copy).then_inc(xT_sb, 1)

            def operands(n, s):
                done(act, q_ps, n)
                done(act, s_ps, n - 2)
                nc.scalar.activation(ka[0:32, s], ps_q[0:32], ACT.Copy)
                nc.scalar.activation(ka[32:64, s], ps_q[32:64], ACT.Square).then_inc(ka_sb, 1)
                done(act, qb_sb, n - 2)
                done(act, ql_sb, n - 2)
                nc.scalar.activation(y[0:32, s], ps_q[0:32], ACT.Copy)
                nc.scalar.activation(y[64:96, s], ps_q[64:96], ACT.Square).then_inc(y_sb, 1)

            def exps(n, s):
                done(act, s_ps, n)
                done(act, av_ps, n - 2)
                nc.scalar.activation(p[:, s], ps_s[:], ACT.Exp, scale=c2).then_inc(p_sb, 1)

            def back(n, s):
                done(act, oT_ps, n)
                done(act, out_ps, n - 1)
                nc.scalar.activation(oT[:], ps_oT[:, 0:128], ACT.Copy).then_inc(oT_sb, 1)

            def step(n, s):
                if plan.has(n + 1):
                    operands(n + 1, 1 - s)
                if plan.has(n):
                    exps(n, s)
                if plan.has(n - 2):
                    back(n - 2, s)
                if plan.has(n + 2):
                    x_rows(n + 2, s)
            plan.run(act, step)

        @block.tensor
        def _(pe):
            nc.tensor.matmul(ps_x[:, 0:128], st.w["a_wq"][:], st.w["a_wv"][:], start=True, stop=True).then_inc(wv_ps, 1)
            pe.wait_ge(wv_sb, 1)
            nc.tensor.matmul(ps_out[:, 0:128], st.w["a_wqT"][:], cbd[:], start=True, stop=True).then_inc(wv_ps, 1)
            pe.wait_ge(wv_sb, 2)
            pe.wait_ge(cst, 6)

            def turn(n, s):
                done(pe, x_sb, n)
                done(pe, xT_sb, n - 1)
                nc.tensor.transpose(ps_x[:, 0:128], x_t[:, s, :], st.ident[:]).then_inc(xT_ps, 1)

            def project(n, s):
                done(pe, xT_sb, n)
                done(pe, y_sb, n - 1)
                for g in range(G):
                    last = nc.tensor.matmul(ps_q[:, g, :], st.w["a_wq3"][:, g, :], xT[:, s, :], start=True, stop=True)
                last.then_inc(q_ps, 1)
                done(pe, v_sb, n - 1)
                nc.tensor.matmul(ps_v[:, 0:128], xT[:, s, :], val[:], start=True, stop=True).then_inc(v_ps, 1)

            def scores(n, s):
                done(pe, ka_sb, n)
                done(pe, qb_sb, n)
                done(pe, ql_sb, n)
                done(pe, p_sb, n - 1)
                for g in range(G):
                    for j in range(2):
                        last = nc.tensor.matmul(
                            ps_s[64 * j:64 * j + 64, g // 2, 256 * (g % 2):256 * (g % 2) + 256],
                            ka[:, s, g, 64 * j:64 * j + 64], qb[:, s, g, :, 64 * j:64 * j + 64],
                            start=True, stop=True)
                last.then_inc(s_ps, 1)

            def attend(n, s):
                done(pe, p_sb, n)
                done(pe, v_sb, n)
                done(pe, o_sb, n - 1)
                pv = p[:, s].rearrange("p a (h t) -> p (a h) t", t=T)
                for h in range(H):
                    last = nc.tensor.matmul(av[64 * (h % 2):64 * (h % 2) + 64, h // 2], pv[:, h, :],
                                            vbd[:, s, h].rearrange("p j e -> p (j e)"), start=True, stop=True)
                last.then_inc(av_ps, 1)

            def turn_back(n, s):
                done(pe, o_sb, n)
                done(pe, oT_sb, n - 1)
                nc.tensor.transpose(ps_oT[:, 0:128], o[:].rearrange("p j q d -> p (j q d)"), st.ident[:]).then_inc(oT_ps, 1)

            def output(n, s):
                done(pe, oT_sb, n)
                done(pe, r_sb, n - 1)
                for hp in range(2):
                    for j in range(2):
                        last = nc.tensor.matmul(ps_out[64 * j:64 * j + 64, 0:128], oT[:, 64 * hp:64 * hp + 64],
                                                st.w["a_outw"][:, j, hp, :], start=hp == 0, stop=hp == 1)
                last.then_inc(out_ps, 1)

            def step(n, s):
                if plan.has(n + 1):
                    project(n + 1, 1 - s)
                if plan.has(n):
                    scores(n, s)
                if plan.has(n - 2):
                    turn_back(n - 2, s)
                if plan.has(n + 2):
                    turn(n + 2, s)
                if plan.has(n - 1):
                    attend(n - 1, 1 - s)
                if plan.has(n - 2):
                    output(n - 2, s)
            plan.run(pe, step)

        @block.vector
        def _(dve):
            nc.vector.memset(ka[64:96], 1.0).then_inc(cst, 1)
            nc.vector.memset(ka[96:128], 0.0).then_inc(cst, 1)
            nc.vector.memset(y[32:64], 1.0).then_inc(cst, 1)
            nc.vector.memset(y[96:128], 0.0).then_inc(cst, 1)
            nc.vector.memset(vbd[:], 0.0).then_inc(cst, 1)
            dve.wait_ge(cst, 5)
            for j in range(2):
                last = nc.vector.memset(vbd[64 * j:64 * j + 64, :, :, j, 8:9], 1.0)
            last.then_inc(cst, 1)
            dve.wait_ge(wv_ps, 1)
            nc.vector.tensor_tensor(cbd[:], ps_x[:, 0:128], st.w["bd8"][:], ALU.mult).then_inc(wv_sb, 1)
            dve.wait_ge(cst, 6)

            def values(n, s):
                done(dve, v_ps, n)
                done(dve, av_ps, n - 2)
                for j in range(2):
                    rows = slice(64 * j, 64 * j + 64)
                    last = nc.vector.tensor_copy(vbd[rows, s, :, j, 0:8],
                                                 ps_v[rows, 0:128].rearrange("p (h d) -> p h d", d=HD))
                last.then_inc(v_sb, 1)

            def masked(n, s):
                done(dve, y_sb, n)
                done(dve, s_ps, n - 2)
                for h in range(HG - 1):
                    last = nc.vector.tensor_scalar(qb[:, s, :, h, :], y[:, s], st.w["a_mask"][:, h:h + 1], None, ALU.mult)
                last.then_inc(qb_sb, 1)

            def normalize(n, s):
                done(dve, av_ps, n)
                done(dve, o_sb, n - 1)
                nc.vector.reciprocal(rec[:], av[:, :, :, 8]).then_inc(rec_sb, 1)
                done(dve, rec_sb, n)
                done(dve, oT_ps, n - 1)
                for j in range(2):
                    last = nc.vector.tensor_tensor(o[:, j], av[:, :, j, 0:8],
                                                   rec[:, :, j:j + 1].to_broadcast([128, 8, HD]), ALU.mult)
                last.then_inc(o_sb, 1)

            def residual(n, s):
                done(dve, out_ps, n)
                done(dve, r_sb, n - 1)
                nc.vector.tensor_tensor(ob[:], ps_out[:, 0:128], st.w["a_outb"][:], ALU.add).then_inc(ob_sb, 1)
                done(dve, ob_sb, n)
                done(dve, x_sb, n)
                nc.vector.tensor_tensor(xa[:, n, :], ob[:], xa[:, n, :], ALU.add).then_inc(r_sb, 1)

            def step(n, s):
                if plan.has(n + 1):
                    masked(n + 1, 1 - s)
                if plan.has(n + 1):
                    values(n + 1, 1 - s)
                if plan.has(n - 1):
                    normalize(n - 1, 1 - s)
                if plan.has(n - 2):
                    residual(n - 2, s)
            plan.run(dve, step)



BANKS = ((0, 6), (6, 12), (12, 16))


def row_max(nc, out, ps_s):
    nc.vector.tensor_reduce(out[:, 0:12], ps_s[:, 0:2, 0:6 * SC].rearrange("p a (h k) -> p a h k", k=SC), AX.X, ALU.max)
    return nc.vector.tensor_reduce(out[:, 12:16], ps_s[:, 2, 0:4 * SC].rearrange("p (h k) -> p h k", k=SC), AX.X, ALU.max)


def subtract_max(nc, out, ps_s, mx):
    for i, (a, b) in enumerate(BANKS):
        last = nc.vector.tensor_tensor(out[:, a:b, :], ps_s[:, i, 0:(b - a) * SC].rearrange("p (h k) -> p h k", k=SC),
                                       mx[:, a:b].unsqueeze(2).to_broadcast([S, b - a, SC]), ALU.subtract)
    return last


def phase_b(nc, st, dram):
    N = B
    plan = Steps(N, 3, 3, 4)
    scale = 1.0 / float(np.sqrt(D))
    with ExitStack() as ctx:
        f = Frame(nc, ctx, "b")
        km = f.sb("km", [S, N, SC], I32)
        xs = f.sb("xs", [S, 2, D])
        cs = f.sb("cs", [SC, 2, D])
        xcT = f.sb("xcT", [D, 2, S + S])
        kp = f.sb("kp", [D, 2, SC])
        kbd = f.sb("kbd", [D, 2, H, SC])
        mb = f.sb("mb", [S, 2, SC], BF16)
        mx = f.sb("mx", [S, 2, H])
        p = f.sb("p", [S, 2, H, SC])
        rs = f.sb("rs", [S, 2, H])
        rc = f.sb("rc", [S, 2, H])
        vpad = f.sb("vpad", [128, 2, 4, 4, 32])
        pT = f.sb("pT", [128, 2, 4, 4, S])
        rT = f.sb("rT", [H, 2, S])
        ou = f.sb("ou", [D, 2, S])
        oT = f.sb("oT", [D, 2, S])
        identb = f.sb("identb", [128, 128], BF16)
        wvo = f.sb("wvo", [D, D])
        gt = f.sb("gt", [D, D])
        bdq, bdk, bdv = (f.sb(n, [D, D]) for n in ("bdq", "bdk", "bdv"))
        ps_s = f.ps("ps_s", [S, 3, 512])
        ps_t = f.ps("ps_t", [SC, 2, 512])
        ps_x, ps_o, ps_r = (f.ps(n, [128, 512]) for n in ("ps_x", "ps_o", "ps_r"))
        (cst, bd_sb, w_ps, w_sb, km_in, xs_sb, xb_sb, cs_sb, x_ps, x_sb, kp_ps, kp_sb, kbd_sb, mb_sb, s_ps,
         mx_sb, sub_sb, p_sb, rs_sb, rc_sb, v_sb, t_ps, t_sb, o_ps, o_sb, rT_ps, rT_sb, r_ps, oT_sb, y_ps, r_sb,
         st_sb) = f.sems(
            "cst", "bd_sb", "w_ps", "w_sb", "km_in", "xs_sb", "xb_sb", "cs_sb", "x_ps", "x_sb", "kp_ps", "kp_sb",
            "kbd_sb", "mb_sb", "s_ps", "mx_sb", "sub_sb", "p_sb", "rs_sb", "rc_sb", "v_sb", "t_ps", "t_sb", "o_ps",
            "o_sb", "rT_ps", "rT_sb", "r_ps", "oT_sb", "y_ps", "r_sb", "st_sb")
        block = f.block()

        @block.sync
        def _(sp):
            sp.dma_start(km[:], dram["kmask"].rearrange("b q k -> q b k")).then_inc(km_in, 16)

        @block.gpsimd
        def _(pool):
            nc.gpsimd.memset(vpad[:], 0.0).then_inc(cst, 1)
            nc.gpsimd.memset(pT[:], 0.0).then_inc(cst, 1)
            nc.gpsimd.memset(xcT[:], 0.0).then_inc(cst, 1)
            pool.wait_ge(cst, 3)

            def context(n, s):
                done(pool, x_ps, n - 2)
                nc.gpsimd.tensor_copy(cs[:, s, :], st.CTX[:, n, :]).then_inc(cs_sb, 1)

            def bias(n, s):
                done(pool, xs_sb, n)
                nc.gpsimd.tensor_tensor(st.X[:, n, :], xs[:, s, :], st.w["b_bo"][:], ALU.add).then_inc(xb_sb, 1)

            def keys(n, s):
                done(pool, kp_sb, n)
                done(pool, s_ps, n - 2)
                nc.gpsimd.tensor_tensor(kbd[:, s], kp[:, s].unsqueeze(1).to_broadcast([D, H, SC]),
                                        st.w["b_head"][:].unsqueeze(2).to_broadcast([D, H, SC]), ALU.mult).then_inc(kbd_sb, 1)

            def values(n, s):
                done(pool, o_ps, n - 2)
                src = st.CTX[:, n, :].rearrange("p (g j d) -> p j g d", j=4, d=HD)
                for j in range(4):
                    last = nc.gpsimd.tensor_copy(vpad[0:SC, s, j, :, HD * j:HD * j + HD], src[:, j])
                last.then_inc(v_sb, 1)

            def step(n, s):
                if plan.has(n + 3):
                    context(n + 3, 1 - s)
                if plan.has(n + 1):
                    keys(n + 1, 1 - s)
                if plan.has(n + 3):
                    bias(n + 3, 1 - s)
                if plan.has(n):
                    values(n, s)
            plan.run(pool, step)

        @block.tensor
        def _(pe):
            pe.wait_ge(bd_sb, 4)
            nc.tensor.matmul(ps_x[:, 0:D], bdk[:], bdq[:], start=True, stop=True).then_inc(w_ps, 1)
            nc.tensor.matmul(ps_o[:, 0:D], bdv[:], st.w["b_woT"][:], start=True, stop=True).then_inc(w_ps, 1)
            pe.wait_ge(w_sb, 2)
            pe.wait_ge(cst, 3)

            def turn(n, s):
                done(pe, xs_sb, n)
                done(pe, cs_sb, n)
                done(pe, kp_sb, n - 1)
                nc.tensor.transpose(ps_x[:, 0:S], xs[:, s, :], st.ident[:])
                nc.tensor.transpose(ps_x[:, S:S + SC], cs[:, s, :], st.ident[0:SC, 0:SC]).then_inc(x_ps, 1)

            def keys(n, s):
                done(pe, x_sb, n)
                nc.tensor.matmul(ps_x[:, 256:256 + 96], gt[:], xcT[:, s, S:S + 96], start=True, stop=True).then_inc(kp_ps, 1)

            def scores(n, s):
                done(pe, kbd_sb, n)
                done(pe, mb_sb, n)
                done(pe, sub_sb, n - 1)
                for i, (a, b) in enumerate(BANKS):
                    out = ps_s[:, i, 0:(b - a) * SC]
                    nc.tensor.matmul(out, xcT[:, s, 0:S], kbd[:, s, a:b, :], start=True, stop=False)
                    last = nc.tensor.matmul(out, identb[:], mb[:, s].unsqueeze(1).to_broadcast([S, b - a, SC]),
                                            start=False, stop=True)
                last.then_inc(s_ps, 1)

            def turn_p(n, s, j):
                if j == 0:
                    done(pe, p_sb, n)
                if j >= 2:
                    pe.wait_ge(t_sb, n * 4 + (j - 1))
                elif plan.has(n - 1) and not (isinstance(n, int) and n == 0):
                    pe.wait_ge(t_sb, n * 4 + (j - 1))
                for g in range(4):
                    last = nc.tensor.transpose(ps_t[:, j % 2, S * g:S * g + S], p[:, s, 4 * g + j, :], st.ident[:])
                last.then_inc(t_ps, 1)

            def attend(n, s, j):
                if j == 0:
                    done(pe, v_sb, n)
                    done(pe, o_sb, n - 1)
                    done(pe, rT_sb, n - 1)
                pe.wait_ge(t_sb, n * 4 + (j + 1))
                for g in range(4):
                    last = nc.tensor.matmul(ps_o[32 * g:32 * g + 32, 0:S], vpad[:, s, j, g, :], pT[:, s, j, g, :],
                                            start=j == 0, stop=j == 3)
                if j == 3:
                    last.then_inc(o_ps, 1)

            def turn_sums(n, s):
                done(pe, rc_sb, n)
                nc.tensor.transpose(ps_o[0:H, 256:256 + S], rc[:, s, :], st.ident[:]).then_inc(rT_ps, 1)

            def spread(n, s):
                done(pe, rT_sb, n)
                done(pe, r_sb, n - 1)
                nc.tensor.matmul(ps_r[:, 0:S], st.w["b_sel"][:], rT[:, s, :], start=True, stop=True).then_inc(r_ps, 1)

            def output(n, s):
                done(pe, oT_sb, n)
                nc.tensor.matmul(ps_r[:, 256:256 + D], oT[:, s, :], wvo[:], start=True, stop=True).then_inc(y_ps, 1)

            def step(n, s):
                if plan.has(n):
                    scores(n, s)
                if plan.has(n + 1):
                    keys(n + 1, 1 - s)
                if plan.has(n - 2):
                    attend(n - 2, s, 3)
                    turn_sums(n - 2, s)
                if plan.has(n - 1):
                    turn_p(n - 1, 1 - s, 0)
                    turn_p(n - 1, 1 - s, 1)
                if plan.has(n + 2):
                    turn(n + 2, s)
                if plan.has(n - 2):
                    spread(n - 2, s)
                if plan.has(n - 1):
                    attend(n - 1, 1 - s, 0)
                    turn_p(n - 1, 1 - s, 2)
                    attend(n - 1, 1 - s, 1)
                    turn_p(n - 1, 1 - s, 3)
                    attend(n - 1, 1 - s, 2)
                if plan.has(n - 2):
                    output(n - 2, s)
            plan.run(pe, step)

        @block.scalar
        def _(act):
            act.wait_ge(w_ps, 2)
            act.wait_ge(cst, 3)
            nc.scalar.activation(gt[:], ps_x[:, 0:D], ACT.Copy).then_inc(w_sb, 1)
            nc.scalar.activation(wvo[:], ps_o[:, 0:D], ACT.Copy).then_inc(w_sb, 1)

            def entry(n, s):
                done(act, x_ps, n - 2)
                done(act, xb_sb, n - 2)
                nc.scalar.activation(xs[:, s, :], st.X[:, n, :], ACT.Identity, scale=st.RSTD[:, bass.ds(n, 1)],
                                     bias=st.SHIFT[:, bass.ds(n, 1)]).then_inc(xs_sb, 1)

            def rows_in(n, s):
                done(act, x_ps, n)
                done(act, s_ps, n - 2)
                nc.scalar.activation(xcT[:, s, 0:S + SC], ps_x[:, 0:S + SC], ACT.Copy).then_inc(x_sb, 1)

            def keys(n, s):
                done(act, kp_ps, n)
                done(act, kbd_sb, n - 2)
                nc.scalar.activation(kp[:, s, :], ps_x[:, 256:256 + SC], ACT.Copy).then_inc(kp_sb, 1)

            def exps(n, s):
                done(act, sub_sb, n)
                flat = p[:, s].rearrange("p h k -> p (h k)")
                nc.scalar.activation(flat, flat, ACT.Exp, scale=scale).then_inc(p_sb, 1)

            def copy_p(n, s, j):
                act.wait_ge(t_ps, n * 4 + (j + 1))
                if j == 0:
                    done(act, o_ps, n - 2)
                nc.scalar.activation(pT[0:SC, s, j].rearrange("p g q -> p (g q)"), ps_t[:, j % 2, :], ACT.Copy).then_inc(t_sb, 1)

            def outputs(n, s):
                done(act, rT_ps, n)
                done(act, oT_sb, n - 2)
                nc.scalar.activation(ou[:, s, :], ps_o[:, 0:S], ACT.Copy).then_inc(o_sb, 1)
                done(act, r_ps, n - 2)
                nc.scalar.activation(rT[:, s, :], ps_o[0:H, 256:256 + S], ACT.Copy).then_inc(rT_sb, 1)

            def step(n, s):
                if plan.has(n + 3):
                    entry(n + 3, 1 - s)
                if plan.has(n + 1):
                    keys(n + 1, 1 - s)
                if plan.has(n - 2):
                    outputs(n - 2, s)
                if plan.has(n - 1):
                    for j in range(4):
                        copy_p(n - 1, 1 - s, j)
                if plan.has(n + 2):
                    rows_in(n + 2, s)
                if plan.has(n):
                    exps(n, s)
            plan.run(act, step)

        @block.vector
        def _(dve):
            for out, w in ((bdq, st.w["b_wq"]), (bdk, st.w["b_wk"]), (bdv, st.w["b_wv"])):
                nc.vector.tensor_tensor(out[:], w[:], st.w["bd8"][:], ALU.mult).then_inc(bd_sb, 1)
            nc.vector.tensor_copy(identb[:], st.ident[:]).then_inc(bd_sb, 1)
            dve.wait_ge(km_in, 16)

            def masks(n, s):
                done(dve, s_ps, n - 2)
                nc.vector.tensor_scalar(mb[:, s, :], km[:, n, :], 0.0, -1e20, ALU.is_equal, ALU.mult).then_inc(mb_sb, 1)

            def sums(n, s):
                done(dve, p_sb, n)
                nc.vector.tensor_reduce(rs[:, s, :], p[:, s], AX.X, ALU.add).then_inc(rs_sb, 1)
                done(dve, rs_sb, n)
                done(dve, rT_ps, n - 2)
                nc.vector.reciprocal(rc[:, s, :], rs[:, s, :]).then_inc(rc_sb, 1)

            def centre(n, s):
                done(dve, s_ps, n)
                row_max(nc, mx[:, s], ps_s).then_inc(mx_sb, 1)
                done(dve, mx_sb, n)
                dve_t = n * 4 - 4
                if not (isinstance(n, int) and n < 2):
                    dve.wait_ge(t_ps, dve_t)
                subtract_max(nc, p[:, s], ps_s, mx[:, s]).then_inc(sub_sb, 1)

            def scaled(n, s):
                done(dve, r_ps, n)
                done(dve, y_ps, n - 2)
                nc.vector.tensor_tensor(oT[:, s, :], ps_r[:, 0:S], ou[:, s, :], ALU.mult).then_inc(oT_sb, 1)

            def residual(n, s):
                done(dve, y_ps, n)
                done(dve, xb_sb, n)
                nc.vector.tensor_tensor(st.X[:, n, :], ps_r[:, 256:256 + D], st.X[:, n, :], ALU.add).then_inc(r_sb, 1)
                done(dve, r_sb, n)
                nc.vector.bn_stats(st.STATS[:, n, :], st.X[:, n, :]).then_inc(st_sb, 1)

            def step(n, s):
                if plan.has(n - 3):
                    residual(n - 3, 1 - s)
                if plan.has(n - 1):
                    sums(n - 1, 1 - s)
                if plan.has(n + 1):
                    masks(n + 1, 1 - s)
                if plan.has(n):
                    centre(n, s)
                if plan.has(n - 2):
                    scaled(n - 2, s)
            plan.run(dve, step)
            done(dve, st_sb, N - 1)



def phase_c(nc, st, dram):
    Q = 4
    W = Q * S
    N = B // Q
    U = E + 2
    plan = Steps(N, 1, 1, 2)
    order = ["e0", "e1", "e2", "e3", "e4", "s2", "e5", "e6", "e7", "e8", "s1", "e9"]
    with ExitStack() as ctx:
        f = Frame(nc, ctx, "c")
        xs = f.sb("xs", [S, Q, D])
        xT = f.sb("xT", [D, W])
        h0 = f.sb("h0", [D, W])
        h1 = f.sb("h1", [D, 2, W])
        sg = f.sb("sg", [D, 2, W])
        gu = f.sb("gu", [D, 2, W])
        lg = f.sb("lg", [S, Q, E])
        top = f.sb("top", [S, Q, E])
        idx = f.sb("idx", [S, Q, E], U32)
        lm = f.sb("lm", [S, Q, E])
        ex = f.sb("ex", [S, Q, E])
        hot = f.sb("hot", [S, Q, TOPK, E])
        sel = f.sb("sel", [S, Q, E])
        wt = f.sb("wt", [S, Q, E])
        ws = f.sb("ws", [S, Q])
        wr = f.sb("wr", [S, Q])
        comb = f.sb("comb", [S, 2, Q, E])
        acc = f.sb("acc", [S, 2, Q, D])
        aT = f.sb("aT", [D, W])
        h2 = f.sb("h2", [D, W])
        fT = f.sb("fT", [D, W])
        ps_a = f.ps("ps_a", [128, 2, 512])
        ps_b = f.ps("ps_b", [128, 2, 512])
        ps_y = f.ps("ps_y", [128, 2, 512])
        ps_t, ps_m = f.ps("ps_t", [128, 512]), f.ps("ps_m", [128, 512])
        (xs_sb, xb_sb, tx_ps, tx_sb, l0_ps, l0_sb, s1_ps, s1_act, s1_sb, g_ps, lg_sb, gv, lm_sb, ex_sb, cb_sb,
         e_ps, e_act, gu_sb, y_ps, acc_sb, ta_ps, ta_sb, l1_ps, l1_sb, s2_ps, s2_act, s2_sb, tf_ps, r_sb,
         st_sb) = f.sems(
            "xs_sb", "xb_sb", "tx_ps", "tx_sb", "l0_ps", "l0_sb", "s1_ps", "s1_act", "s1_sb", "g_ps", "lg_sb", "gv",
            "lm_sb", "ex_sb", "cb_sb", "e_ps", "e_act", "gu_sb", "y_ps", "acc_sb", "ta_ps", "ta_sb", "l1_ps",
            "l1_sb", "s2_ps", "s2_act", "s2_sb", "tf_ps", "r_sb", "st_sb")
        block = f.block()
        GV = 9
        tile = lambda n: bass.ds(n * Q, Q)

        def item(n, name):
            return n - 1 if name == "s2" else n + 1 if name == "s1" else n

        def wait_pair(eng, n, name):
            at = order.index(name) - 2
            while True:
                m, other = n + at // len(order), order[at % len(order)]
                i = item(m, other)
                if plan.has(i):
                    break
                if i < 0 and m < 0:
                    return
                at -= 2
            if other == "s1":
                done(eng, s1_sb, i)
            elif other == "s2":
                done(eng, s2_sb, i)
            else:
                eng.wait_ge(gu_sb, i * U + int(other[1:]) + 1)

        @block.gpsimd
        def _(pool):
            def step(n, s):
                if plan.has(n + 1):
                    done(pool, xs_sb, n + 1)
                    nc.gpsimd.tensor_copy(st.X[:, tile(n + 1), :], xs[:]).then_inc(xb_sb, 1)
            plan.run(pool, step)

        @block.tensor
        def _(pe):
            def four_turns(out, src, sem):
                for q in range(Q):
                    last = nc.tensor.transpose(out[:, S * q:S * q + S], src(q), st.ident[:])
                last.then_inc(sem, 1)

            def pair(n, s, name, w1, w2, rhs, sem):
                bank = order.index(name) % 2
                wait_pair(pe, n, name)
                nc.tensor.matmul(ps_a[:, bank, :], w1, rhs, start=True, stop=True)
                nc.tensor.matmul(ps_b[:, bank, :], w2, rhs, start=True, stop=True).then_inc(sem, 1)

            def up(n, s, u):
                if u == 0:
                    done(pe, s1_sb, n)
                pair(n, s, f"e{u}", st.w["c_w1"][:, u, :], st.w["c_w3"][:, u, :], h1[:, s, :], e_ps)

            def down(n, s, u):
                shared = u == U - 2
                pe.wait_ge(gu_sb, n * U + (u + 1 + shared))
                if u >= 2:
                    pe.wait_ge(acc_sb, n * 9 + (u - 1))
                elif u == 0 and not (isinstance(n, int) and n == 0):
                    pe.wait_ge(acc_sb, n * 9)
                for q in range(Q):
                    for k in range(1 + shared):
                        last = nc.tensor.matmul(ps_y[:, u % 2, D * q:D * q + D], gu[:, (u + k) % 2, S * q:S * q + S],
                                                st.w["c_w2"][:, u + k, :], start=k == 0, stop=k == shared)
                last.then_inc(y_ps, 1)

            def step(n, s):
                m, ms = n - 1, 1 - s
                k, ks = n + 1, 1 - s
                if plan.has(n):
                    up(n, s, 0)
                if plan.has(m):
                    down(m, ms, U - 2)
                if plan.has(n):
                    up(n, s, 1)
                    down(n, s, 0)
                    up(n, s, 2)
                if plan.has(m):
                    done(pe, acc_sb, m, 9)
                    done(pe, tx_sb, n if plan.has(n) else m)
                    done(pe, r_sb, m - 1)
                    four_turns(ps_t, lambda q: acc[:, ms, q, :], ta_ps)
                if plan.has(n):
                    down(n, s, 1)
                    up(n, s, 3)
                if plan.has(m):
                    done(pe, ta_sb, m)
                    done(pe, lg_sb, n if plan.has(n) else m)
                    nc.tensor.matmul(ps_m[:], st.w["c_lin1"][:], aT[:], start=True, stop=True).then_inc(l1_ps, 1)
                if plan.has(n):
                    down(n, s, 2)
                    up(n, s, 4)
                if plan.has(m):
                    done(pe, l1_sb, m)
                    pair(n, s, "s2", st.w["c_s2w1"][:], st.w["c_s2w2"][:], h2[:], s2_ps)
                if plan.has(n):
                    down(n, s, 3)
                    up(n, s, 5)
                if plan.has(m):
                    done(pe, s2_sb, m)
                    four_turns(ps_t, lambda q: fT[:, S * q:S * q + S], tf_ps)
                if plan.has(n):
                    down(n, s, 4)
                    up(n, s, 6)
                if plan.has(k):
                    done(pe, xs_sb, k)
                    done(pe, r_sb, m)
                    done(pe, tx_sb, n)
                    four_turns(ps_t, lambda q: xs[:, q, :], tx_ps)
                if plan.has(n):
                    down(n, s, 5)
                    up(n, s, 7)
                if plan.has(k):
                    done(pe, tx_sb, k)
                    done(pe, l1_sb, m)
                    done(pe, lg_sb, n)
                    nc.tensor.matmul(ps_m[:], st.w["c_lin0"][:], xT[:], start=True, stop=True).then_inc(l0_ps, 1)
                if plan.has(n):
                    down(n, s, 6)
                    up(n, s, 8)
                if plan.has(k):
                    done(pe, l0_sb, k)
                    pair(n, s, "s1", st.w["c_s1w1"][:], st.w["c_s1w2"][:], h0[:], s1_ps)
                if plan.has(n):
                    down(n, s, 7)
                    up(n, s, 9)
                if plan.has(k):
                    done(pe, s1_sb, k)
                    for q in range(Q):
                        last = nc.tensor.matmul(ps_m[:, E * q:E * q + E], h1[:, ks, S * q:S * q + S], st.w["c_gate"][:],
                                                start=True, stop=True)
                    last.then_inc(g_ps, 1)
            plan.run(pe, step)

        @block.scalar
        def _(act):
            def silu(n, u):
                act.wait_ge(e_ps, n * U + (u + 1))
                bank = order.index(f"e{u}") % 2
                nc.scalar.activation(sg[:, bank, :], ps_a[:, bank, :], ACT.Silu).then_inc(e_act, 1)

            def step(n, s):
                m, k = n - 1, n + 1
                for u in range(3):
                    if plan.has(n):
                        silu(n, u)
                if plan.has(m):
                    done(act, ta_ps, m)
                    nc.scalar.activation(aT[:], ps_t[:], ACT.Copy).then_inc(ta_sb, 1)
                if plan.has(n):
                    silu(n, 3)
                if plan.has(m):
                    done(act, l1_ps, m)
                    nc.scalar.activation(h2[:], ps_m[:], ACT.Identity, bias=st.w["c_lin1b"][:]).then_inc(l1_sb, 1)
                if plan.has(n):
                    silu(n, 4)
                if plan.has(m):
                    done(act, s2_ps, m)
                    bank = order.index("s2") % 2
                    nc.scalar.activation(sg[:, bank, :], ps_a[:, bank, :], ACT.Silu, bias=st.w["c_s2b1"][:]).then_inc(s2_act, 1)
                for u in range(5, 7):
                    if plan.has(n):
                        silu(n, u)
                if plan.has(k):
                    done(act, tx_ps, k)
                    nc.scalar.activation(xT[:], ps_t[:], ACT.Copy).then_inc(tx_sb, 1)
                if plan.has(n):
                    silu(n, 7)
                if plan.has(k):
                    done(act, l0_ps, k)
                    nc.scalar.activation(h0[:], ps_m[:], ACT.Identity, bias=st.w["c_lin0b"][:]).then_inc(l0_sb, 1)
                if plan.has(n):
                    silu(n, 8)
                if plan.has(k):
                    done(act, s1_ps, k)
                    bank = order.index("s1") % 2
                    nc.scalar.activation(sg[:, bank, :], ps_a[:, bank, :], ACT.Silu, bias=st.w["c_s1b1"][:]).then_inc(s1_act, 1)
                if plan.has(n):
                    silu(n, 9)
                if plan.has(k):
                    done(act, lm_sb, k)
                    nc.scalar.activation(ex[:], lm[:], ACT.Exp).then_inc(ex_sb, 1)
            plan.run(act, step)

        @block.vector
        def _(dve):
            def entry(n):
                done(dve, tx_ps, n - 1)
                done(dve, xb_sb, n - 1)
                for q in range(Q):
                    at = bass.ds(n * Q + q, 1)
                    last = nc.vector.tensor_scalar(xs[:, q, :], st.X[:, n * Q + q, :], st.MEAN[:, at], st.RSTD[:, at],
                                                   ALU.subtract, ALU.mult)
                last.then_inc(xs_sb, 1)

            def gated(n, u):
                dve.wait_ge(e_act, n * U + (u + 1))
                if u >= 2:
                    dve.wait_ge(y_ps, n * 9 + (u - 1))
                elif not (isinstance(n, int) and n == 0):
                    dve.wait_ge(y_ps, n * 9)
                bank = order.index(f"e{u}") % 2
                nc.vector.tensor_tensor(gu[:, u % 2, :], ps_b[:, bank, :], sg[:, bank, :], ALU.mult).then_inc(gu_sb, 1)

            def weigh(n, s, u):
                dve.wait_ge(y_ps, n * 9 + (u + 1))
                if u == 0:
                    done(dve, cb_sb, n)
                    done(dve, ta_ps, n - 2)
                else:
                    dve.wait_ge(acc_sb, n * 9 + u)
                for q in range(Q):
                    y, a = ps_y[:, u % 2, D * q:D * q + D], acc[:, s, q, :]
                    if u == 0:
                        last = nc.vector.tensor_scalar(a, y, comb[:, s, q, 0:1], None, ALU.mult)
                    elif u < E:
                        last = nc.vector.scalar_tensor_tensor(out=a, in0=y, scalar=comb[:, s, q, u:u + 1], in1=a,
                                                              op0=ALU.mult, op1=ALU.add)
                if u == E:
                    flat = acc[:, s].rearrange("p q d -> p (q d)")
                    last = nc.vector.tensor_tensor(flat, ps_y[:, 0, :], flat, ALU.add)
                last.then_inc(acc_sb, 1)

            def choose(n, s):
                done(dve, g_ps, n)
                nc.vector.tensor_copy(lg[:].rearrange("p q e -> p (q e)"), ps_m[:, 0:Q * E]).then_inc(lg_sb, 1)
                done(dve, lg_sb, n)
                nc.vector.tensor_reduce(ws[:], lg[:], AX.X, ALU.max).then_inc(gv, 1)
                for q in range(Q):
                    last = nc.vector.max(top[:, q, :], lg[:, q, :])
                last.then_inc(gv, 1)
                dve.wait_ge(gv, n * GV + 1)
                done(dve, ex_sb, n - 1)
                nc.vector.tensor_tensor(lm[:], lg[:], ws[:].unsqueeze(2).to_broadcast([S, Q, E]), ALU.subtract).then_inc(lm_sb, 1)
                dve.wait_ge(gv, n * GV + 2)
                nc.vector.tensor_copy(wt[:], top[:]).then_inc(gv, 1)
                for q in range(Q):
                    last = nc.vector.max_index(idx[:, q, :], top[:, q, :], lg[:, q, :])
                last.then_inc(gv, 1)
                dve.wait_ge(gv, n * GV + 4)
                nc.vector.tensor_tensor(hot[:], idx[:, :, 0:TOPK].unsqueeze(3).to_broadcast([S, Q, TOPK, E]),
                                        st.w["c_iota"][:].rearrange("p (k e) -> p k e", k=TOPK).unsqueeze(1).to_broadcast([S, Q, TOPK, E]),
                                        ALU.is_equal).then_inc(gv, 1)
                dve.wait_ge(gv, n * GV + 5)
                nc.vector.tensor_reduce(sel[:], hot[:].rearrange("p q k e -> p q e k"), AX.X, ALU.add).then_inc(gv, 1)
                done(dve, ex_sb, n)
                dve.wait_ge(gv, n * GV + 6)
                nc.vector.tensor_tensor(wt[:], ex[:], sel[:], ALU.mult).then_inc(gv, 1)
                dve.wait_ge(gv, n * GV + 7)
                nc.vector.tensor_reduce(ws[:], wt[:], AX.X, ALU.add).then_inc(gv, 1)
                dve.wait_ge(gv, n * GV + 8)
                nc.vector.reciprocal(wr[:], ws[:]).then_inc(gv, 1)
                dve.wait_ge(gv, n * GV + 9)
                nc.vector.tensor_tensor(comb[:, s], wt[:], wr[:].unsqueeze(2).to_broadcast([S, Q, E]), ALU.mult).then_inc(cb_sb, 1)

            def swiglu(out, name, b2, sem):
                bank = order.index(name) % 2
                nc.vector.scalar_tensor_tensor(out=out, in0=ps_b[:, bank, :], scalar=b2, in1=sg[:, bank, :],
                                               op0=ALU.add, op1=ALU.mult).then_inc(sem, 1)

            def step(n, s):
                m, ms, k, ks = n - 1, 1 - s, n + 1, 1 - s
                if plan.has(k):
                    entry(k)
                if plan.has(n):
                    gated(n, 0)
                if plan.has(m):
                    weigh(m, ms, E)
                if plan.has(n):
                    for u in range(1, 5):
                        gated(n, u)
                        weigh(n, s, u - 1)
                if plan.has(m):
                    done(dve, s2_act, m)
                    swiglu(fT[:], "s2", st.w["c_s2b2"][:], s2_sb)
                if plan.has(n):
                    gated(n, 5)
                    weigh(n, s, 4)
                if plan.has(m):
                    done(dve, tf_ps, m)
                    done(dve, xb_sb, m)
                    nc.vector.tensor_tensor(st.X[:, tile(m), :], ps_t[:].rearrange("p (q d) -> p q d", q=Q),
                                            st.X[:, tile(m), :], ALU.add).then_inc(r_sb, 1)
                    done(dve, r_sb, m)
                    for q in range(Q):
                        last = nc.vector.bn_stats(st.STATS[:, m * Q + q, :], st.X[:, m * Q + q, :])
                    last.then_inc(st_sb, 1)
                if plan.has(n):
                    for u in range(6, 9):
                        gated(n, u)
                        weigh(n, s, u - 1)
                if plan.has(k):
                    done(dve, s1_act, k)
                    swiglu(h1[:, ks, :], "s1", st.w["c_s1b2"][:], s1_sb)
                if plan.has(n):
                    gated(n, 9)
                if plan.has(k):
                    choose(k, ks)
            plan.run(dve, step)
            done(dve, st_sb, N - 1)



def phase_d(nc, st, dram):
    Q = 2
    N = B // Q
    plan = Steps(N, 3, 3, 4)
    with ExitStack() as ctx:
        f = Frame(nc, ctx, "d")
        xs = f.sb("xs", [S, 2, Q, D])
        xT = f.sb("xT", [D, 2, Q, S])
        qk = f.sb("qk", [S, 2, Q, 2 * H, HD])
        qkm = f.sb("qkm", [S, 2, Q, 2 * H, HD])
        mx = f.sb("mx", [S, 2, Q, 2 * H])
        qke = f.sb("qke", [S, 2, Q, 2 * D])
        v1 = f.sb("v1", [S, 2, Q, D + H])
        qT = f.sb("qT", [D, 2, Q, S])
        kvbd = f.sb("kvbd", [D, 2, Q, D + H])
        den = f.sb("den", [S, Q, H])
        rec = f.sb("rec", [S, Q, H])
        y = f.sb("y", [S, 2, Q, D])
        yT = f.sb("yT", [D, 2, Q, S])
        ps_x, ps_qT, ps_kv, ps_y, ps_yT, ps_o = (
            f.ps(n, [128, 512]) for n in ("ps_x", "ps_qT", "ps_kv", "ps_y", "ps_yT", "ps_o"))
        ps_p = f.ps("ps_p", [128, Q, 512])
        (cst, xs_sb, xb_sb, xT_ps, xT_sb, p_ps, b_sb, mx_sb, qkm_sb, qke_sb, kv_ps, qT_ps, qT_sb, kv_sb,
         y_ps, den_sb, rec_sb, y_sb, yT_ps, yT_sb, o_ps, r_sb, st_sb) = f.sems(
            "cst", "xs_sb", "xb_sb", "xT_ps", "xT_sb", "p_ps", "b_sb", "mx_sb", "qkm_sb", "qke_sb", "kv_ps",
            "qT_ps", "qT_sb", "kv_sb", "y_ps", "den_sb", "rec_sb", "y_sb", "yT_ps", "yT_sb", "o_ps", "r_sb",
            "st_sb")
        block = f.block()
        tile = lambda n: bass.ds(n * Q, Q)
        kv = ps_kv[:, 0:Q * (D + H)].rearrange("p (q c) -> p q c", q=Q)
        my = ps_y[:, 0:Q * (D + H)].rearrange("p (q c) -> p q c", q=Q)
        all_of = lambda t, s: t[:, s].rearrange("p q c -> p (q c)")

        @block.gpsimd
        def _(pool):
            def centre(n, s):
                done(pool, mx_sb, n)
                done(pool, qke_sb, n - 2)
                nc.gpsimd.tensor_tensor(qkm[:, s].rearrange("p q h d -> p (q h) d"), qk[:, s].rearrange("p q h d -> p (q h) d"),
                                        mx[:, s].rearrange("p q h -> p (q h)").unsqueeze(2).to_broadcast([S, Q * 2 * H, HD]),
                                        ALU.subtract).then_inc(qkm_sb, 1)

            def step(n, s):
                if plan.has(n + 1):
                    centre(n + 1, 1 - s)
                if plan.has(n + 2):
                    done(pool, xs_sb, n + 2)
                    nc.gpsimd.tensor_tensor(st.X[:, tile(n + 2), :], xs[:, s], st.w["d_bo"][:].unsqueeze(1).to_broadcast([S, Q, D]),
                                            ALU.add).then_inc(xb_sb, 1)
            plan.run(pool, step)

        @block.tensor
        def _(pe):
            def turn(n, s):
                done(pe, xs_sb, n)
                done(pe, xT_sb, n - 1)
                for q in range(Q):
                    last = nc.tensor.transpose(ps_x[:, S * q:S * q + S], xs[:, s, q, :], st.ident[:])
                last.then_inc(xT_ps, 1)

            def project(n, s):
                done(pe, xT_sb, n)
                done(pe, b_sb, n - 1)
                for q in range(Q):
                    last = nc.tensor.matmul(ps_p[:, q, 0:3 * D], xT[:, s, q, :], st.w["d_wqkv"][:], start=True, stop=True)
                last.then_inc(p_ps, 1)

            def outer(n, s):
                done(pe, qke_sb, n)
                done(pe, kv_sb, n - 1)
                for q in range(Q):
                    last = nc.tensor.matmul(kv[:, q], qke[:, s, q, D:2 * D], v1[:, s, q, :], start=True, stop=True)
                last.then_inc(kv_ps, 1)
                done(pe, qT_sb, n - 1)
                for q in range(Q):
                    last = nc.tensor.transpose(ps_qT[:, S * q:S * q + S], qke[:, s, q, 0:D], st.ident[:])
                last.then_inc(qT_ps, 1)

            def mix(n, s):
                done(pe, qT_sb, n)
                done(pe, kv_sb, n)
                done(pe, y_sb, n - 1)
                for q in range(Q):
                    last = nc.tensor.matmul(my[:, q], qT[:, s, q, :], kvbd[:, s, q], start=True, stop=True)
                last.then_inc(y_ps, 1)

            def turn_back(n, s):
                done(pe, y_sb, n)
                done(pe, yT_sb, n - 1)
                for q in range(Q):
                    last = nc.tensor.transpose(ps_yT[:, S * q:S * q + S], y[:, s, q, :], st.ident[:])
                last.then_inc(yT_ps, 1)

            def output(n, s):
                done(pe, yT_sb, n)
                done(pe, r_sb, n - 1)
                for q in range(Q):
                    last = nc.tensor.matmul(ps_o[:, D * q:D * q + D], yT[:, s, q, :], st.w["d_wo"][:], start=True, stop=True)
                last.then_inc(o_ps, 1)

            def step(n, s):
                if plan.has(n + 1):
                    project(n + 1, 1 - s)
                if plan.has(n - 1):
                    mix(n - 1, 1 - s)
                if plan.has(n + 2):
                    turn(n + 2, s)
                if plan.has(n - 2):
                    turn_back(n - 2, s)
                if plan.has(n):
                    outer(n, s)
                if plan.has(n - 2):
                    output(n - 2, s)
            plan.run(pe, step)

        @block.scalar
        def _(act):
            def entry(n, s):
                done(act, xT_ps, n - 2)
                done(act, xb_sb, n - 2)
                for q in range(Q):
                    at = bass.ds(n * Q + q, 1)
                    last = nc.scalar.activation(xs[:, s, q, :], st.X[:, n * Q + q, :], ACT.Identity,
                                                scale=st.RSTD[:, at], bias=st.SHIFT[:, at])
                last.then_inc(xs_sb, 1)

            def exps(n, s):
                done(act, qkm_sb, n)
                done(act, kv_ps, n - 2)
                done(act, qT_ps, n - 2)
                nc.scalar.activation(all_of(qke, s), qkm[:, s].rearrange("p q h d -> p (q h d)"), ACT.Exp).then_inc(qke_sb, 1)

            def x_rows(n, s):
                done(act, xT_ps, n)
                done(act, p_ps, n - 2)
                nc.scalar.activation(all_of(xT, s), ps_x[:, 0:Q * S], ACT.Copy).then_inc(xT_sb, 1)

            def q_rows(n, s):
                done(act, qT_ps, n)
                done(act, y_ps, n - 2)
                nc.scalar.activation(all_of(qT, s), ps_qT[:, 0:Q * S], ACT.Copy).then_inc(qT_sb, 1)

            def y_rows(n, s):
                done(act, yT_ps, n)
                done(act, o_ps, n - 2)
                nc.scalar.activation(all_of(yT, s), ps_yT[:, 0:Q * S], ACT.Copy).then_inc(yT_sb, 1)

            def step(n, s):
                if plan.has(n + 2):
                    x_rows(n + 2, s)
                if plan.has(n - 2):
                    y_rows(n - 2, s)
                if plan.has(n):
                    q_rows(n, s)
                if plan.has(n + 3):
                    entry(n + 3, 1 - s)
                if plan.has(n + 1):
                    exps(n + 1, 1 - s)
            plan.run(act, step)

        @block.vector
        def _(dve):
            nc.vector.memset(v1[:, :, :, D:D + H], 1.0).then_inc(cst, 1)
            dve.wait_ge(cst, 1)

            def biased(n, s):
                done(dve, p_ps, n)
                done(dve, kv_ps, n - 2)
                nc.vector.tensor_tensor(v1[:, s, :, 0:D], ps_p[:, :, 2 * D:3 * D],
                                        st.w["d_bqkv"][:, 2 * D:3 * D].unsqueeze(1).to_broadcast([S, Q, D]), ALU.add)
                done(dve, qkm_sb, n - 1)
                nc.vector.tensor_tensor(qk[:, s].rearrange("p q h d -> p q (h d)"), ps_p[:, :, 0:2 * D],
                                        st.w["d_bqkv"][:, 0:2 * D].unsqueeze(1).to_broadcast([S, Q, 2 * D]), ALU.add).then_inc(b_sb, 1)

            def maxima(n, s):
                done(dve, b_sb, n)
                nc.vector.tensor_reduce(mx[:, s].rearrange("p q h -> p (q h)"), qk[:, s].rearrange("p q h d -> p (q h) d"), AX.X, ALU.max).then_inc(mx_sb, 1)

            def diagonal(n, s):
                done(dve, kv_ps, n)
                done(dve, y_ps, n - 2)
                nc.vector.tensor_tensor(kvbd[:, s], kv, st.w["d_bd"][:].unsqueeze(1).to_broadcast([D, Q, D + H]), ALU.mult).then_inc(kv_sb, 1)

            def denominators(n, s):
                done(dve, y_ps, n)
                done(dve, rec_sb, n - 1)
                nc.vector.tensor_scalar(den[:], my[:, :, D:D + H], 1e-6, None, ALU.add).then_inc(den_sb, 1)

            def inverses(n, s):
                done(dve, den_sb, n)
                done(dve, y_sb, n - 1)
                nc.vector.reciprocal(rec[:], den[:]).then_inc(rec_sb, 1)

            def divide(n, s):
                done(dve, rec_sb, n)
                done(dve, yT_ps, n - 2)
                nc.vector.tensor_tensor(y[:, s].rearrange("p q (h d) -> p q h d", d=HD),
                                        my[:, :, 0:D].rearrange("p q (h d) -> p q h d", d=HD),
                                        rec[:].unsqueeze(3).to_broadcast([S, Q, H, HD]), ALU.mult).then_inc(y_sb, 1)

            def residual(n, s):
                done(dve, o_ps, n)
                done(dve, xb_sb, n)
                nc.vector.tensor_tensor(st.X[:, tile(n), :], ps_o[:, 0:Q * D].rearrange("p (q d) -> p q d", q=Q),
                                        st.X[:, tile(n), :], ALU.add).then_inc(r_sb, 1)

            def stats(n, s):
                done(dve, r_sb, n)
                for q in range(Q):
                    last = nc.vector.bn_stats(st.STATS[:, n * Q + q, :], st.X[:, n * Q + q, :])
                last.then_inc(st_sb, 1)

            def step(n, s):
                if plan.has(n + 1):
                    biased(n + 1, 1 - s)
                if plan.has(n - 1):
                    denominators(n - 1, 1 - s)
                if plan.has(n + 1):
                    maxima(n + 1, 1 - s)
                if plan.has(n - 1):
                    inverses(n - 1, 1 - s)
                if plan.has(n):
                    diagonal(n, s)
                if plan.has(n - 1):
                    divide(n - 1, 1 - s)
                if plan.has(n - 2):
                    residual(n - 2, s)
                    stats(n - 2, s)
            plan.run(dve, step)
            done(dve, st_sb, N - 1)



def phase_e(nc, st, dram):
    N = B
    PAIRS = H // 2
    plan = Steps(N, 4, 2, 4, unroll=4)
    KC = ((0, 3), (3, 6), (6, 8))
    with ExitStack() as ctx:
        f = Frame(nc, ctx, "e")
        g = f.sb("g", [D, H, D])
        xs = f.sb("xs", [S, 2, D])
        cs = f.sb("cs", [SC, 2, D])
        xT = f.sb("xT", [D, 4, S])
        cT = f.sb("cT", [D, 4, SC])
        kk = f.sb("kk", [D, 2, H, 2, SC])
        v = f.sb("v", [128, 4, H * DK])
        mx = f.sb("mx", [S, 2, H])
        p = f.sb("p", [S, 2, H, SC])
        pn = f.sb("pn", [S, 2, H, SC])
        rs = f.sb("rs", [S, 2, H])
        rc = f.sb("rc", [S, 2, H])
        pT = f.sb("pT", [128, H, S])
        oT = f.sb("oT", [128, 2, PAIRS, S])
        half = f.sb("half", [S, D])
        ps_s = f.ps("ps_s", [S, 3, 512])
        ps_o = f.ps("ps_o", [128, 2, 512])
        ps_t, ps_k, ps_x = (f.ps(n, [128, 512]) for n in ("ps_t", "ps_k", "ps_x"))
        (cst, g_ps, g_sb, xs_sb, xb_sb, cs_sb, x_ps, x_sb, k_ps, k_sb, v_ps, v_sb, vb_sb, s_ps, mx_sb, sub_sb, p_sb,
         rs_sb, rc_sb, pn_sb, t_ps, t_sb, o_ps, o_sb, y_ps, half_sb, r_sb,
         st_sb) = f.sems(
            "cst", "g_ps", "g_sb", "xs_sb", "xb_sb", "cs_sb", "x_ps", "x_sb", "k_ps", "k_sb", "v_ps", "v_sb", "vb_sb",
            "s_ps", "mx_sb", "sub_sb", "p_sb", "rs_sb", "rc_sb", "pn_sb", "t_ps", "t_sb", "o_ps", "o_sb", "y_ps",
            "half_sb", "r_sb", "st_sb")
        block = f.block()
        g_banks = [ps_s[:, 0], ps_s[:, 1], ps_s[:, 2], ps_o[:, 0]]

        @block.gpsimd
        def _(pool):
            nc.gpsimd.memset(pT[:], 0.0).then_inc(cst, 1)
            nc.gpsimd.memset(v[:], 0.0).then_inc(cst, 1)
            pool.wait_ge(cst, 2)

            def context(n, s):
                done(pool, x_ps, n - 2)
                nc.gpsimd.tensor_copy(cs[:, s % 2, :], st.CTX[:, n, :]).then_inc(cs_sb, 1)

            def keep(n, s):
                done(pool, xs_sb, n)
                nc.gpsimd.tensor_copy(st.X[:, n, :], xs[:, s % 2, :]).then_inc(xb_sb, 1)

            def normalize(n, s):
                done(pool, rc_sb, n)
                done(pool, t_ps, n - 2, 4)
                nc.gpsimd.tensor_tensor(pn[:, s % 2], p[:, s % 2], rc[:, s % 2].unsqueeze(2).to_broadcast([S, H, SC]),
                                        ALU.mult).then_inc(pn_sb, 1)

            def step(n, s):
                if plan.has(n + 4):
                    context(n + 4, s)
                    keep(n + 4, s)
                if plan.has(n):
                    normalize(n, s)
            plan.run(pool, step)

        @block.tensor
        def _(pe):
            for h in range(H):
                last = nc.tensor.matmul(g_banks[h // 4][:, D * (h % 4):D * (h % 4) + D], st.w["e_wkT"][:, h, :],
                                        st.w["e_wqT"][:, h, :], start=True, stop=True)
                if h % 4 == 3:
                    last.then_inc(g_ps, 1)
            pe.wait_ge(g_sb, H // 4)
            pe.wait_ge(cst, 2)

            def turn(n, s):
                done(pe, xs_sb, n)
                done(pe, cs_sb, n)
                done(pe, x_sb, n - 1)
                done(pe, r_sb, n - 6)
                nc.tensor.transpose(ps_x[:, 0:S], xs[:, s % 2, :], st.ident[:])
                nc.tensor.transpose(ps_x[:, S:S + SC], cs[:, s % 2, :], st.ident[0:SC, 0:SC]).then_inc(x_ps, 1)

            def keys(n, s, c):
                a, b = KC[c]
                if c == 0:
                    done(pe, x_sb, n + 1 - s % 2)
                    done(pe, v_sb, n - 2)
                    if isinstance(n, int) and n == 1:
                        done(pe, k_sb, 0, 3)
                else:
                    pe.wait_ge(k_sb, n * 3 + c)
                for h in range(a, b):
                    last = nc.tensor.matmul(ps_k[:, (h - a) * 2 * SC:(h - a + 1) * 2 * SC], g[:, 8 * (s % 2) + h, :],
                                            cT[:, s - s % 2:s - s % 2 + 2, :].rearrange("p w k -> p (w k)"), start=True, stop=True)
                last.then_inc(k_ps, 1)

            def values(n, s, c):
                if c == 0:
                    if not isinstance(n, int) or n + 1 < N:
                        done(pe, k_sb, n + 1, 3)
                    else:
                        done(pe, v_sb, n - 1)
                    done(pe, x_sb, n)
                else:
                    done(pe, t_sb, n - 2, 4)
                    if isinstance(n, int) and 0 < n < 2:
                        done(pe, vb_sb, n - 1)
                nc.tensor.matmul((ps_k, ps_t)[c][0:SC, :], cT[:, s, :], st.w["e_wv"][:, 512 * c:512 * c + 512], start=True, stop=True).then_inc(v_ps, 1)

            def scores(n, s):
                done(pe, k_sb, n + 1 - s % 2, 3)
                done(pe, x_sb, n)
                done(pe, sub_sb, n - 1)
                for i, (a, b) in enumerate(BANKS):
                    last = nc.tensor.matmul(ps_s[:, i, 0:(b - a) * SC], xT[:, s, :], kk[:, s // 2, a:b, s % 2, :],
                                            start=True, stop=True)
                last.then_inc(s_ps, 1)

            def turn_p(n, s, c):
                if c == 0:
                    done(pe, pn_sb, n)
                    done(pe, t_sb, n - 1, 4)
                    if not isinstance(n, int) or n + 1 < N:
                        done(pe, vb_sb, n + 1)
                else:
                    pe.wait_ge(t_sb, n * 4 + c)
                for h in range(4):
                    last = nc.tensor.transpose(ps_t[0:SC, S * h:S * h + S], pn[:, s % 2, 4 * c + h, :], st.ident[:])
                last.then_inc(t_ps, 1)

            def attend(n, s, c):
                if c == 0:
                    done(pe, v_sb, n)
                    done(pe, vb_sb, n)
                if c % 2 == 0 and not (isinstance(n, int) and n == 0):
                    pe.wait_ge(o_sb, n * 2 - 1 + c // 2)
                pe.wait_ge(t_sb, n * 4 + (c + 1))
                for h in range(4 * c, 4 * c + 4):
                    col = S * (h // 2 % 4)
                    last = nc.tensor.matmul(ps_o[64 * (h % 2):64 * (h % 2) + 64, c // 2, col:col + S],
                                            v[:, s, DK * h:DK * h + DK], pT[:, h, :], start=True, stop=True)
                if c % 2 == 1:
                    last.then_inc(o_ps, 1)

            def output(n, s, half):
                pe.wait_ge(o_sb, n * 2 + (half + 1))
                if half == 0:
                    done(pe, r_sb, n - 1)
                rows = n + 4 + half
                if not isinstance(n, int) or rows < N:
                    done(pe, x_sb, rows)
                else:
                    done(pe, x_sb, N - 1)
                for c in range(4 * half, 4 * half + 4):
                    last = nc.tensor.matmul(ps_x[:, 256 + D * half:256 + D * half + D], oT[:, s % 2, c, :],
                                            st.w["e_wo"][:, c, :], start=c % 4 == 0, stop=c % 4 == 3)
                if half == 1:
                    last.then_inc(y_ps, 1)

            def step(n, s):
                m, ms = n - 1, (s - 1) % 4
                kn, ks = n + 2, (s + 2) % 4
                if plan.has(n):
                    scores(n, s)
                if plan.has(n - 2):
                    output(n - 2, (s - 2) % 4, 1)
                if plan.has(m):
                    turn_p(m, ms, 0)
                if plan.has(kn):
                    keys(kn, ks, 0)
                if plan.has(m):
                    turn_p(m, ms, 1)
                    attend(m, ms, 0)
                if plan.has(kn):
                    keys(kn, ks, 1)
                if plan.has(m):
                    turn_p(m, ms, 2)
                    attend(m, ms, 1)
                if plan.has(kn):
                    keys(kn, ks, 2)
                if plan.has(m):
                    turn_p(m, ms, 3)
                    attend(m, ms, 2)
                    output(m, ms, 0)
                if plan.has(n + 1):
                    values(n + 1, (s + 1) % 4, 0)
                if plan.has(m):
                    attend(m, ms, 3)
                if plan.has(n + 4):
                    turn(n + 4, s)
                if plan.has(n + 1):
                    values(n + 1, (s + 1) % 4, 1)
            plan.run(pe, step)

        @block.scalar
        def _(act):
            for i, bank in enumerate(g_banks):
                act.wait_ge(g_ps, i + 1)
                nc.scalar.activation(g[:, 4 * i:4 * i + 4, :].rearrange("p h d -> p (h d)"), bank, ACT.Copy).then_inc(g_sb, 1)

            def rows_in(n, s):
                done(act, x_ps, n)
                done(act, s_ps, n - 4)
                nc.scalar.activation(xT[:, s, :], ps_x[:, 0:S], ACT.Copy)
                done(act, v_ps, n - 4, 2)
                done(act, k_ps, n + 1 - s % 2 - 4, 3)
                nc.scalar.activation(cT[:, s, :], ps_x[:, S:S + SC], ACT.Copy).then_inc(x_sb, 1)

            def copy_keys(n, s, c):
                a, b = KC[c]
                act.wait_ge(k_ps, n * 3 + (c + 1))
                if c == 0:
                    done(act, s_ps, n - s % 2 - 3)
                half = 8 * (s % 2)
                nc.scalar.activation(kk[:, s // 2, half + a:half + b].rearrange("p h w k -> p (h w k)"),
                                     ps_k[:, 0:(b - a) * 2 * SC], ACT.Copy).then_inc(k_sb, 1)

            def exps(n, s, half):
                done(act, sub_sb, n)
                flat = p[:, s % 2, 8 * half:8 * half + 8].rearrange("p h k -> p (h k)")
                last = nc.scalar.activation(flat, flat, ACT.Exp, scale=1.0 / float(np.sqrt(DK)))
                if half == 1:
                    last.then_inc(p_sb, 1)

            def copy_p(n, s, c):
                act.wait_ge(t_ps, n * 4 + (c + 1))
                if c == 0:
                    done(act, o_ps, n - 1, 2)
                nc.scalar.activation(pT[0:SC, 4 * c:4 * c + 4].rearrange("p h q -> p (h q)"), ps_t[0:SC, :], ACT.Copy).then_inc(t_sb, 1)

            def copy_values(n, s):
                act.wait_ge(v_ps, n * 2 + 1)
                done(act, o_ps, n - 4, 2)
                nc.scalar.activation(v[0:SC, s, 0:512], ps_k[0:SC, :], ACT.Copy).then_inc(v_sb, 1)

            def outputs(n, s, c):
                act.wait_ge(o_ps, n * 2 + (c + 1))
                done(act, y_ps, n - 2)
                nc.scalar.activation(oT[:, s % 2, 4 * c:4 * c + 4].rearrange("p h q -> p (h q)"), ps_o[:, c, :], ACT.Copy).then_inc(o_sb, 1)

            def step(n, s):
                m, ms = n - 1, (s - 1) % 4
                kn, ks = n + 2, (s + 2) % 4
                if plan.has(m):
                    copy_p(m, ms, 0)
                if plan.has(kn):
                    copy_keys(kn, ks, 0)
                if plan.has(m):
                    copy_p(m, ms, 1)
                if plan.has(n):
                    exps(n, s, 0)
                if plan.has(kn):
                    copy_keys(kn, ks, 1)
                if plan.has(m):
                    copy_p(m, ms, 2)
                    outputs(m, ms, 0)
                if plan.has(n):
                    exps(n, s, 1)
                if plan.has(kn):
                    copy_keys(kn, ks, 2)
                if plan.has(m):
                    copy_p(m, ms, 3)
                if plan.has(n + 1):
                    copy_values(n + 1, (s + 1) % 4)
                if plan.has(m):
                    outputs(m, ms, 1)
                if plan.has(n + 4):
                    rows_in(n + 4, s)
            plan.run(act, step)

        @block.vector
        def _(dve):
            dve.wait_ge(cst, 2)

            def entry(n, s):
                done(dve, x_ps, n - 2)
                done(dve, xb_sb, n - 2)
                nc.vector.tensor_scalar(xs[:, s % 2, :], st.X[:, n, :], st.MEAN[:, bass.ds(n, 1)], st.RSTD[:, bass.ds(n, 1)],
                                        ALU.subtract, ALU.mult).then_inc(xs_sb, 1)

            def copy_values(n, s):
                done(dve, v_ps, n, 2)
                done(dve, o_ps, n - 4, 2)
                nc.vector.tensor_copy(v[0:SC, s, 512:1024], ps_t[0:SC, :]).then_inc(vb_sb, 1)

            def centre(n, s):
                done(dve, s_ps, n)
                row_max(nc, mx[:, s % 2], ps_s).then_inc(mx_sb, 1)
                done(dve, mx_sb, n)
                done(dve, pn_sb, n - 2)
                subtract_max(nc, p[:, s % 2], ps_s, mx[:, s % 2]).then_inc(sub_sb, 1)

            def sums(n, s):
                done(dve, p_sb, n)
                nc.vector.tensor_reduce(rs[:, s % 2, :], p[:, s % 2], AX.X, ALU.add).then_inc(rs_sb, 1)
                done(dve, rs_sb, n)
                nc.vector.reciprocal(rc[:, s % 2, :], rs[:, s % 2, :]).then_inc(rc_sb, 1)

            def residual(n, s):
                done(dve, y_ps, n)
                done(dve, xb_sb, n)
                done(dve, r_sb, n - 1)
                nc.vector.tensor_tensor(half[:], ps_x[:, 256:256 + D], st.X[:, n, :], ALU.add).then_inc(half_sb, 1)
                done(dve, half_sb, n)
                nc.vector.tensor_tensor(st.X[:, n, :], ps_x[:, 256 + D:256 + 2 * D], half[:], ALU.add).then_inc(r_sb, 1)
                done(dve, r_sb, n)
                nc.vector.bn_stats(st.STATS[:, n, :], st.X[:, n, :]).then_inc(st_sb, 1)

            def step(n, s):
                if plan.has(n + 4):
                    entry(n + 4, s)
                if plan.has(n):
                    centre(n, s)
                if plan.has(n - 2):
                    residual(n - 2, (s - 2) % 4)
                if plan.has(n):
                    sums(n, s)
                if plan.has(n + 1):
                    copy_values(n + 1, (s + 1) % 4)
            plan.run(dve, step)
            done(dve, st_sb, N - 1)



K16, KC = 16, 15
FF = 512
FAR = -1e30
TWO_PI = 2.0 * float(np.pi)
PI_HI = 6.28125
PI_MID = float(np.float32(np.round((TWO_PI - PI_HI) * 2.0 ** 22) / 2.0 ** 22))
PI_LO = TWO_PI - PI_HI - PI_MID
ROUND = 1.5 * 2.0 ** 23
PI_SAFE = 3.1415925


def phase_f(nc, st, dram):
    GROUPS, PG, NB = 8, 2, 8
    PARTS = GROUPS // PG
    R = NB * K16
    KINDS = 4
    BD = NB * (R + K16)
    CHUNKS = 8
    CW, LOW = B // CHUNKS, 3
    BY_VECTOR = (0, 3, 6)
    with ExitStack() as ctx:
        f = Frame(nc, ctx, "mod")
        w = {}
        first, items = [], []
        for name, ap in dram.items():
            if name.startswith("f_"):
                shape = list(ap.shape)
                if name in SPREAD:
                    shape[0] = 128
                w[name[2:]] = t = f.sb("w" + name, shape, ap.dtype)
                (first if "router" in name else items).append((t[:], ap.broadcast_to(shape) if name in SPREAD else ap))
        scratch = dram["scratch"]
        wt = f.sb("wt", [S, B])
        ident = st.ident
        wT = f.sb("wT", [B, S])
        wT2 = f.sb("wT2", [B, S])
        top = f.sb("top", [B, K16])
        idx = f.sb("idx", [B, K16], U32)
        pack = f.sb("pack", [B, 2 * K16])
        packed = f.sb("packed", [S, B, 2 * K16])
        G = f.sb("G", [S, GROUPS, R])
        keep = f.sb("keep", [S, B])
        pos = f.sb("pos", [S, KINDS])
        ang = f.sb("ang", [S, 2, KINDS, 4])
        turns = f.sb("turns", [S, 2, KINDS, 4])
        red = f.sb("red", [S, 2, KINDS, 4])
        cs = f.sb("cs", [S, 2 * KINDS * 4])
        MT = f.sb("MT", [S, GROUPS, R])
        GM = f.sb("GM", [S, 2, PG, BD])
        qM = f.sb("qM", [D, 2, PG, BD])
        GT = f.sb("GT", [R, 2, PG, S])
        xsel = f.sb("xsel", [R, 2, PG, D])
        sq = f.sb("sq", [R, 2, PG, D])
        csk = f.sb("csk", [R, 2, PG, 2 * KINDS * 4])
        csr = f.sb("csr", [R, 2, PG, 2, 4])
        wM = f.sb("wM", [R, 2, PG, NB])
        mk = f.sb("mk", [R, 2, PG, NB, K16])
        msel = f.sb("msel", [R, 2, PG, K16])
        ms = f.sb("ms", [R, 2, PG])
        var = f.sb("var", [R, 2, PG])
        std = f.sb("std", [R, 2, PG])
        rs = f.sb("rs", [R, 2, PG])
        hn = f.sb("hn", [R, 2, PG, D])
        hT = f.sb("hT", [D, 2, PG * R])
        qc = f.sb("qc", [R, 2, PG, 2 * H, 2, 4])
        qs = f.sb("qs", [R, 2, PG, 2 * H, 2, 4])
        qk = f.sb("qk", [R, 2, PG, 2, H, 2, 4])
        v = f.sb("v", [R, 2, PG, D])
        kT = f.sb("kT", [D, 2, PG * R])
        kM = f.sb("kM", [D, 2, PG, NB, H, K16])
        VM = f.sb("VM", [128, 2, NB, PG, D])
        sc = f.sb("sc", [R, 2, PG, H, K16])
        sm = f.sb("sm", [R, 2, PG, H, K16])
        mx = f.sb("mx", [R, 2, PG, H])
        su = f.sb("su", [R, 2, PG, H])
        ru = f.sb("ru", [R, 2, PG, H])
        PT = f.sb("PT", [128, 2, PG, 2, R])
        oT = f.sb("oT", [D, 2, PG, R])
        x1 = f.sb("x1", [R, 2, PG, D])
        gT = kM[:].rearrange("p s g b h k -> p s (g b h k)")[:, :, 0:FF // 128 * PG * R].rearrange("p s (c r) -> p s c r", c=FF // 128)
        x2 = f.sb("x2", [R, 2, PG, D])
        prod = kM[:].rearrange("p s g b h k -> p (s g b h k)").rearrange("p (c b d) -> p c b d", c=CHUNKS, d=D)
        ps = f.ps("ps", [128, 2, 4, 512])
        (router_in, landed, zeroed, v1, pe1, act1, pk_sb, pk_out, pk_in, g_sb, mt_ps, mt_sb, w_sb, ang_sb,
         low, high, mine, others, wsum,
         gm_sb, ga_ps, xs_sb, sel_sb, ms_sb, std_sb, rs_sb, hn_sb, ht_ps, ht_sb, qkv_ps, v_sb, ro, qk_sb, qkT_ps, qT_sb,
         km_sb, ka_sb, kp_sb, va_ps, va_sb, vb_ps, vb_sb, s_ps, sv, sm_sb, e_sb, pn_sb, pT_ps, PT_sb, o_ps, oT_sb, y_ps, x1_sb,
         sq2_sb, ms2_sb, std2_sb, rs2_sb, hn2_sb, ht2_ps, ht2_sb, h1_ps, gT_sb, h2_ps, x2_sb, pm_sb, sc_ps, xk_sb,
         r_sb, st_sb) = f.sems(
            "router_in", "landed", "zeroed", "v1", "pe1", "act1", "pk_sb", "pk_out", "pk_in", "g_sb", "mt_ps", "mt_sb", "w_sb", "ang_sb",
            "low", "high", "mine", "others", "wsum",
            "gm_sb", "ga_ps", "xs_sb", "sel_sb", "ms_sb", "std_sb", "rs_sb", "hn_sb", "ht_ps", "ht_sb", "qkv_ps", "v_sb", "ro",
            "qk_sb", "qkT_ps", "qT_sb", "km_sb", "ka_sb", "kp_sb", "va_ps", "va_sb", "vb_ps", "vb_sb", "s_ps", "sv", "sm_sb", "e_sb", "pn_sb",
            "pT_ps", "PT_sb", "o_ps", "oT_sb", "y_ps", "x1_sb", "sq2_sb", "ms2_sb", "std2_sb", "rs2_sb", "hn2_sb",
            "ht2_ps", "ht2_sb", "h1_ps", "gT_sb", "h2_ps", "x2_sb", "pm_sb", "sc_ps", "xk_sb", "r_sb", "st_sb")
        block = f.block()
        pairs = [(0, 1), (2, 3)]

        def diag(t, s, g):
            return t[:, s, g, :].rearrange("p (b c) -> p b c", b=NB)[:, :, 0:K16]

        def spread_keys(eng, s, a, b):
            return eng.tensor_tensor(kM[:, s, :, :, a:b].rearrange("p g b h k -> p (g b) h k"),
                                     kT[:, s].rearrange("p (b k) -> p b k", k=K16).unsqueeze(2).to_broadcast([D, PG * NB, b - a, K16]),
                                     w["head"][:, a:b].unsqueeze(1).unsqueeze(3).to_broadcast([D, PG * NB, b - a, K16]), ALU.mult)

        @block.sync
        def _(sp):
            for dst, src in first:
                sp.dma_start(dst, src).then_inc(router_in, 16)
            for dst, src in items:
                sp.dma_start(dst, src).then_inc(landed, 16)
            sp.wait_ge(pk_sb, 1)
            sp.dma_start(scratch[:], pack[:]).then_inc(pk_out, 16)
            sp.wait_ge(pk_out, 16)
            flat = scratch.rearrange("b k -> (b k)").unsqueeze(0).broadcast_to([S, B * 2 * K16])
            sp.dma_start(packed[:].rearrange("p b k -> p (b k)"), flat).then_inc(pk_in, 16)

        @block.gpsimd
        def _(pool):
            pool.wait_ge(router_in, 16 * len(first))
            for c in range(CHUNKS):
                if c not in BY_VECTOR:
                    pool.wait_ge(low, LOW * (c + 1))
                    pool.wait_ge(high, (CW - LOW) * (c + 1))
                    nc.gpsimd.tensor_tensor(prod[:, c], st.X[:, CW * c:CW * c + CW, :],
                                            w["router"][:].unsqueeze(1).to_broadcast([S, CW, D]), ALU.mult).then_inc(others, 1)
            nc.gpsimd.memset(GM[:], 0.0).then_inc(zeroed, 1)
            nc.gpsimd.memset(qM[:], 0.0).then_inc(zeroed, 1)
            for pair in pairs:
                for p in pair:
                    done(pool, ga_ps, p)
                    pool.wait_ge(g_sb, 2)
                    b = slice(NB * PG * p, NB * PG * p + NB * PG)
                    nc.gpsimd.tensor_tensor(st.X[:, b, :], st.X[:, b, :],
                                            keep[:, b].unsqueeze(2).to_broadcast([S, NB * PG, D]), ALU.mult).then_inc(xk_sb, 1)
                for p in pair:
                    done(pool, qT_sb, p)
                    done(pool, h2_ps, p - 2)
                    spread_keys(nc.gpsimd, p % 2, 12, 16).then_inc(kp_sb, 1)

        @block.vector
        def _(dve):
            vec = nc.vector
            n = 0

            def seq(ins):
                nonlocal n
                n += 1
                ins.then_inc(v1, 1)

            def settle():
                dve.wait_ge(v1, n)
            def router_sum(c):
                if c in BY_VECTOR:
                    dve.wait_ge(mine, BY_VECTOR.index(c) + 1)
                else:
                    dve.wait_ge(others, len([i for i in range(c + 1) if i not in BY_VECTOR]))
                vec.tensor_reduce(wt[:, CW * c:CW * c + CW], prod[:, c], AX.X, ALU.add).then_inc(wsum, 1)
            for c in range(CHUNKS):
                for b in range(CW * c, CW * c + LOW):
                    vec.tensor_scalar(st.X[:, b, :], st.X[:, b, :], st.MEAN[:, b:b + 1], st.RSTD[:, b:b + 1],
                                      ALU.subtract, ALU.mult).then_inc(low, 1)
                if c in BY_VECTOR:
                    dve.wait_ge(router_in, 16 * len(first))
                    dve.wait_ge(low, LOW * (c + 1))
                    dve.wait_ge(high, (CW - LOW) * (c + 1))
                    vec.tensor_tensor(prod[:, c], st.X[:, CW * c:CW * c + CW, :],
                                      w["router"][:].unsqueeze(1).to_broadcast([S, CW, D]), ALU.mult).then_inc(mine, 1)
                if c >= 2:
                    router_sum(c - 2)
            router_sum(CHUNKS - 2)
            router_sum(CHUNKS - 1)
            dve.wait_ge(wsum, CHUNKS)
            vec.tensor_scalar(wt[:], wt[:], w["routerb"][:], None, ALU.add).then_inc(w_sb, 1)
            dve.wait_ge(pe1, 1)
            seq(vec.tensor_copy(wT[:], ps[0:B, 0, 0, 0:S]))
            settle()
            seq(vec.max(top[:, 0:8], wT[:]))
            settle()
            seq(vec.match_replace(wT2[:], top[:, 0:8], wT[:], -3e38))
            seq(vec.max_index(idx[:, 0:8], top[:, 0:8], wT[:]))
            settle()
            seq(vec.max(top[:, 8:16], wT2[:]))
            settle()
            seq(vec.max_index(idx[:, 8:16], top[:, 8:16], wT2[:]))
            seq(vec.tensor_copy(pack[:, K16:2 * K16], top[:]))
            settle()
            seq(vec.tensor_copy(pack[:, 0:K16], idx[:]))
            settle()
            vec.memset(pack[:, KC:K16], -1.0).then_inc(pk_sb, 1)
            dve.wait_ge(landed, 16 * len(items))
            seq(vec.tensor_copy(pos[:], w["pos"][:]))
            settle()
            for half in range(2):
                seq(vec.tensor_tensor(ang[:, half], pos[:].unsqueeze(2).to_broadcast([S, KINDS, 4]),
                                      w["inv"][:].unsqueeze(1).to_broadcast([S, KINDS, 4]), ALU.mult))
            settle()
            for half in range(2):
                seq(vec.tensor_scalar(turns[:, half], ang[:, half], 1.0 / TWO_PI, 0.25 * (1 - half), ALU.mult, ALU.add))
            settle()
            seq(vec.tensor_scalar(red[:], turns[:], ROUND, None, ALU.add))
            settle()
            seq(vec.tensor_scalar(turns[:], red[:], ROUND, None, ALU.subtract))
            settle()
            for c in (PI_HI, PI_MID, PI_LO):
                seq(vec.scalar_tensor_tensor(out=ang[:], in0=turns[:], scalar=-c, in1=ang[:], op0=ALU.mult, op1=ALU.add))
                settle()
            for half in range(2):
                seq(vec.tensor_scalar(red[:, half], ang[:, half], 0.5 * float(np.pi) * (1 - half), PI_SAFE, ALU.add, ALU.min))
            settle()
            vec.tensor_scalar(turns[:], red[:], -PI_SAFE, None, ALU.max).then_inc(ang_sb, 1)
            dve.wait_ge(pk_in, 16)
            vec.tensor_scalar(G[:].rearrange("p g (b k) -> p (g b) k", k=K16), packed[:, :, 0:K16], w["token"][:], None,
                              ALU.is_equal).then_inc(g_sb, 1)
            seq(vec.tensor_tensor(keep[:], wt[:], packed[:, :, 2 * K16 - 1], ALU.is_le))
            settle()
            vec.tensor_scalar(keep[:], keep[:], 1.0, None, ALU.add).then_inc(g_sb, 1)
            dve.wait_ge(g_sb, 2)
            dve.wait_ge(zeroed, 2)

            def square_mean(s, src, q, sem):
                seq(vec.tensor_reduce(ms[:, s], q, AX.X, ALU.add))
                settle()
                vec.tensor_scalar(var[:, s], ms[:, s], 1.0 / D, 1e-6, ALU.mult, ALU.add).then_inc(sem, 1)

            def scale_rows(p, s, src, std_sem, rs_sem, sem):
                done(dve, std_sem, p)
                vec.reciprocal(rs[:, s], std[:, s]).then_inc(rs_sem, 1)
                done(dve, rs_sem, p)
                vec.tensor_tensor(hn[:, s], src, rs[:, s].unsqueeze(2).to_broadcast([R, PG, D]), ALU.mult).then_inc(sem, 1)

            for pair in pairs:
                for p in pair:
                    s = p % 2
                    done(dve, ga_ps, p - 2)
                    for g in range(PG):
                        last = vec.tensor_copy(diag(GM, s, g), G[:, PG * p + g, :].rearrange("p (b k) -> p b k", b=NB))
                    last.then_inc(gm_sb, 1)
                for p in pair:
                    s = p % 2
                    done(dve, ga_ps, p)
                    seq(vec.tensor_tensor(wM[:, s], ps[:, s, 1, PG * (R + 32):PG * (R + 32) + PG * NB].rearrange("p (g b) -> p g b", g=PG),
                                          w["own"][:].unsqueeze(1).to_broadcast([R, PG, NB]), ALU.mult))
                    for g in range(PG):
                        seq(vec.tensor_tensor(csk[:, s, g].rearrange("p (h k i) -> p h k i", h=2, i=4),
                                              ps[:, s, 1, PG * R + 32 * g:PG * R + 32 * g + 32].rearrange("p (h k i) -> p h k i", h=2, i=4),
                                              w["kind"][:, PG * p + g].unsqueeze(1).unsqueeze(3).to_broadcast([R, 2, KINDS, 4]), ALU.mult))
                    seq(vec.tensor_tensor(mk[:, s], ps[:, s, 1, 0:PG * R].rearrange("p (g b k) -> p g b k", g=PG, k=K16),
                                          w["own"][:].unsqueeze(1).unsqueeze(3).to_broadcast([R, PG, NB, K16]), ALU.mult))
                    settle()
                    seq(vec.tensor_reduce(csr[:, s].rearrange("p g h i -> p (g h) i"),
                                          csk[:, s].rearrange("p g (h k i) -> p (g h) i k", h=2, i=4), AX.X, ALU.add))
                    seq(vec.tensor_reduce(msel[:, s], mk[:, s].rearrange("p g b k -> p g k b"), AX.X, ALU.add))
                    settle()
                    vec.memset(msel[:, s, :, KC:K16], FAR).then_inc(sel_sb, 1)
                    done(dve, xs_sb, p)
                    square_mean(s, xsel, sq[:, s], ms_sb)
                for p in pair:
                    scale_rows(p, p % 2, xsel[:, p % 2], std_sb, rs_sb, hn_sb)
                for p in pair:
                    s = p % 2
                    done(dve, ht_ps, p)
                    vec.tensor_scalar(hT[:, s], ps[:, s, 3, 0:PG * R], w["ln1"][:], None, ALU.mult).then_inc(ht_sb, 1)
                for p in pair:
                    s = p % 2
                    done(dve, qkv_ps, p)
                    done(dve, sel_sb, p)
                    src = ps[:, s, 0, :].rearrange("p (g e i) -> p g e i", g=PG, i=4)
                    for dst, which in ((qc, 0), (qs, 1)):
                        seq(vec.tensor_tensor(dst[:, s].rearrange("p g h t i -> p g (h t) i"), src,
                                              csr[:, s, :, which].unsqueeze(2).to_broadcast([R, PG, 4 * H, 4]), ALU.mult))
                    settle()
                    rot = qk[:, s].rearrange("p g w h t i -> p (g w h) t i")
                    c, r = (t[:, s].rearrange("p g h t i -> p (g h) t i") for t in (qc, qs))
                    seq(vec.tensor_tensor(rot[:, :, 0], c[:, :, 0], r[:, :, 1], ALU.subtract))
                    vec.tensor_tensor(rot[:, :, 1], c[:, :, 1], r[:, :, 0], ALU.add).then_inc(qk_sb, 1)
                for p in pair:
                    s = p % 2
                    for half, ready_sem, sem in ((0, va_ps, va_sb), (1, vb_ps, vb_sb)):
                        done(dve, ready_sem, p)
                        for j in range(2):
                            b0 = 4 * half + 2 * j
                            last = vec.tensor_tensor(VM[:, s, b0:b0 + 2].rearrange("p b g (h d) -> p (b g) h d", h=2),
                                                     ps[:, s, j, :].rearrange("p (b h d) -> p b h d", h=2, d=D // 2),
                                                     w["vown"][:].unsqueeze(1).unsqueeze(1).to_broadcast([128, 2 * PG, 2, D // 2]), ALU.mult)
                        last.then_inc(sem, 1)
                        if half == 0:
                            done(dve, qT_sb, p)
                            spread_keys(vec, s, 0, 8).then_inc(km_sb, 1)
                for p in pair:
                    s = p % 2
                    done(dve, s_ps, p)
                    flat = lambda t: t[:, s].rearrange("p g h k -> p (g h) k")
                    for g in range(PG):
                        seq(vec.scalar_tensor_tensor(out=sc[:, s, g], in0=ps[:, s, 3, 256 * g:256 * g + 256].rearrange("p (h k) -> p h k", k=K16),
                                                     scalar=1.0 / float(np.sqrt(HD)),
                                                     in1=msel[:, s, g].unsqueeze(1).to_broadcast([R, H, K16]), op0=ALU.mult, op1=ALU.add))
                    settle()
                    seq(vec.tensor_reduce(mx[:, s].rearrange("p g h -> p (g h)"), flat(sc), AX.X, ALU.max))
                    settle()
                    vec.tensor_tensor(sm[:, s], sc[:, s], mx[:, s].unsqueeze(3).to_broadcast([R, PG, H, K16]), ALU.subtract).then_inc(sm_sb, 1)
                for p in pair:
                    s = p % 2
                    flat = lambda t: t[:, s].rearrange("p g h k -> p (g h) k")
                    done(dve, e_sb, p)
                    seq(vec.tensor_reduce(su[:, s].rearrange("p g h -> p (g h)"), flat(sc), AX.X, ALU.add))
                    settle()
                    seq(vec.reciprocal(ru[:, s], su[:, s]))
                    settle()
                    vec.tensor_tensor(sm[:, s], sc[:, s], ru[:, s].unsqueeze(3).to_broadcast([R, PG, H, K16]), ALU.mult).then_inc(pn_sb, 1)
                for p in pair:
                    s = p % 2
                    done(dve, y_ps, p)
                    vec.tensor_tensor(x1[:, s], ps[:, s, 2, 0:PG * D].rearrange("p (g d) -> p g d", g=PG), xsel[:, s], ALU.add).then_inc(x1_sb, 1)
                    done(dve, sq2_sb, p)
                    square_mean(s, x1, sq[:, s], ms2_sb)
                for p in pair:
                    scale_rows(p, p % 2, x1[:, p % 2], std2_sb, rs2_sb, hn2_sb)
                for p in pair:
                    s = p % 2
                    done(dve, ht2_ps, p)
                    vec.tensor_scalar(hT[:, s], ps[:, s, 3, 0:PG * R], w["ln2"][:], None, ALU.mult).then_inc(ht2_sb, 1)
                for p in pair:
                    s = p % 2
                    done(dve, h2_ps, p)
                    vec.tensor_tensor(x2[:, s], ps[:, s, 2, 0:PG * D].rearrange("p (g d) -> p g d", g=PG), x1[:, s], ALU.add).then_inc(x2_sb, 1)
                    done(dve, x2_sb, p)
                    vec.tensor_tensor(VM[:, s].rearrange("p b g d -> p g b d"), x2[:, s].unsqueeze(2).to_broadcast([R, PG, NB, D]),
                                      wM[:, s].unsqueeze(3).to_broadcast([R, PG, NB, D]), ALU.mult).then_inc(pm_sb, 1)
                for p in pair:
                    s = p % 2
                    done(dve, sc_ps, p)
                    done(dve, xk_sb, p)
                    b = NB * PG * p
                    for i in range(4):
                        at = slice(b + 4 * i, b + 4 * i + 4)
                        last = vec.tensor_tensor(st.X[:, at, :], ps[:, s, i, :].rearrange("p (b d) -> p b d", b=4), st.X[:, at, :], ALU.add)
                    last.then_inc(r_sb, 1)
                    dve.wait_ge(r_sb, p + 1)
                    for i in range(NB * PG):
                        vec.bn_stats(st.STATS[:, b + i, :], st.X[:, b + i, :]).then_inc(st_sb, 1)
            dve.wait_ge(st_sb, B)

        @block.scalar
        def _(act):
            copy = lambda dst, src: nc.scalar.activation(dst, src, ACT.Copy)
            for c in range(CHUNKS):
                for b in range(CW * c + LOW, CW * c + CW):
                    nc.scalar.activation(st.X[:, b, :], st.X[:, b, :], ACT.Identity, scale=st.RSTD[:, b:b + 1],
                                         bias=st.SHIFT[:, b:b + 1]).then_inc(high, 1)
            act.wait_ge(ang_sb, 1)
            nc.scalar.activation(cs[:], turns[:].rearrange("p h k i -> p (h k i)"), ACT.Sin).then_inc(act1, 1)
            for half in range(2):
                act.wait_ge(mt_ps, half + 1)
                copy(MT[:, 4 * half:4 * half + 4].rearrange("p g r -> p (g r)"), ps[:, 1, half, :]).then_inc(mt_sb, 1)
            for pair in pairs:
                for p in pair:
                    s = p % 2
                    done(act, ga_ps, p)
                    copy(xsel[:, s].rearrange("p g d -> p (g d)"), ps[:, s, 0, 0:PG * D])
                    nc.scalar.activation(sq[:, s].rearrange("p g d -> p (g d)"), ps[:, s, 0, 0:PG * D], ACT.Square)
                    copy(GT[:, s].rearrange("p g t -> p (g t)"), ps[:, s, 2, 0:PG * S]).then_inc(xs_sb, 1)
                for p in pair:
                    done(act, ms_sb, p)
                    nc.scalar.activation(std[:, p % 2], var[:, p % 2], ACT.Sqrt).then_inc(std_sb, 1)
                for p in pair:
                    s = p % 2
                    done(act, qkv_ps, p)
                    copy(v[:, s].rearrange("p g d -> p (g d)"), ps[:, s, 1, 0:PG * D]).then_inc(v_sb, 1)
                for p in pair:
                    s = p % 2
                    done(act, qkT_ps, p)
                    src = ps[:, s, 2, :].rearrange("p (g w b k) -> p g w b k", g=PG, w=2, k=K16)
                    for g in range(PG):
                        copy(diag(qM, s, g), src[:, g, 0])
                    copy(kT[:, s].rearrange("p (g c) -> p g c", g=PG), ps[:, s, 2, :].rearrange("p (g w c) -> p g w c", g=PG, w=2)[:, :, 1]).then_inc(qT_sb, 1)
                for p in pair:
                    s = p % 2
                    done(act, qT_sb, p)
                    done(act, h2_ps, p - 2)
                    for h in range(8, 12):
                        last = nc.scalar.activation(kM[:, s, :, :, h].rearrange("p g b k -> p (g b) k"),
                                                    kT[:, s].rearrange("p (b k) -> p b k", k=K16), ACT.Copy, scale=w["head"][:, h:h + 1])
                    last.then_inc(ka_sb, 1)
                for p in pair:
                    s = p % 2
                    done(act, sm_sb, p)
                    nc.scalar.activation(sc[:, s].rearrange("p g h k -> p (g h k)"), sm[:, s].rearrange("p g h k -> p (g h k)"), ACT.Exp).then_inc(e_sb, 1)
                for p in pair:
                    s = p % 2
                    done(act, pT_ps, p)
                    copy(PT[:, s].rearrange("p g a r -> p (g a r)"), ps[:, s, 2, :]).then_inc(PT_sb, 1)
                for p in pair:
                    s = p % 2
                    done(act, o_ps, p)
                    copy(oT[:, s].rearrange("p g r -> p (g r)"), ps[:, s, 3, 0:PG * R]).then_inc(oT_sb, 1)
                for p in pair:
                    s = p % 2
                    done(act, x1_sb, p)
                    nc.scalar.activation(sq[:, s].rearrange("p g d -> p (g d)"), x1[:, s].rearrange("p g d -> p (g d)"), ACT.Square).then_inc(sq2_sb, 1)
                for p in pair:
                    done(act, ms2_sb, p)
                    nc.scalar.activation(std[:, p % 2], var[:, p % 2], ACT.Sqrt).then_inc(std2_sb, 1)
                for p in pair:
                    s = p % 2
                    for i in range(2):
                        act.wait_ge(h1_ps, 2 * p + i + 1)
                        nc.scalar.activation(gT[:, s, 2 * i:2 * i + 2].rearrange("p c r -> p (c r)"), ps[:, s, i, :],
                                             ACT.Gelu_apprx_tanh).then_inc(gT_sb, 1)

        @block.tensor
        def _(pe):
            mm = nc.tensor.matmul
            TURNS = (0, 2, 4, 6, 1, 3, 5, 7)
            pe.wait_ge(w_sb, 1)
            nc.tensor.transpose(ps[0:B, 0, 0, 0:S], wt[:], ident[:]).then_inc(pe1, 1)
            pe.wait_ge(landed, 16 * len(items))
            pe.wait_ge(g_sb, 2)
            for half in range(2):
                first = 3 * K16 if half == 0 else 0
                cols = G[:, 4 * half:4 * half + 4].rearrange("p g r -> p (g r)")
                last = mm(ps[:, 1, half, first:512], w["amask"][:, KINDS - 1, :], cols[:, first:512], start=True, stop=True)
                if half == 0:
                    for k in range(KINDS - 1):
                        last = mm(ps[:, 1, 0, K16 * k:K16 * k + K16], w["amask"][:, k, :], cols[:, K16 * k:K16 * k + K16], start=True, stop=True)
                last.then_inc(mt_ps, 1)
            pe.wait_ge(act1, 1)
            pe.wait_ge(mt_sb, 2)
            for pair in pairs:
                for p in pair:
                    s = p % 2
                    done(pe, gm_sb, p)
                    done(pe, r_sb, p - 2)
                    for g in range(PG):
                        gr = PG * p + g
                        for b in TURNS:
                            rows = slice(b // 2 * 32, b // 2 * 32 + 32)
                            mm(ps[rows, s, 0, D * g:D * g + D], GM[:, s, g, R * b + rows.start:R * b + rows.stop],
                               st.X[:, NB * gr + b, :], start=b % 2 == 0, stop=b % 2 == 1)
                        mm(ps[:, s, 1, PG * R + 32 * g:PG * R + 32 * g + 32], G[:, gr, :], cs[:], start=True, stop=True)
                        at = PG * (R + 32) + NB * g
                        mm(ps[:, s, 1, at:at + NB], G[:, gr, :], wt[:, NB * gr:NB * gr + NB], start=True, stop=True)
                        mm(ps[:, s, 1, R * g:R * g + R], MT[:, gr, :], G[:, gr, :], start=True, stop=True)
                        last = nc.tensor.transpose(ps[:, s, 2, S * g:S * g + S], G[:, gr, :], ident[:])
                    last.then_inc(ga_ps, 1)
                for p in pair:
                    s = p % 2
                    done(pe, hn_sb, p)
                    for g in range(PG):
                        last = nc.tensor.transpose(ps[:, s, 3, R * g:R * g + R], hn[:, s, g, :], ident[:])
                    last.then_inc(ht_ps, 1)
                for p in pair:
                    s = p % 2
                    done(pe, ht_sb, p)
                    done(pe, sel_sb, p)
                    done(pe, xs_sb, p)
                    for g in range(PG):
                        mm(ps[:, s, 0, 2 * D * g:2 * D * g + 2 * D], hT[:, s, R * g:R * g + R], w["wqkv"][:, 0:2 * D], start=True, stop=True)
                        last = mm(ps[:, s, 1, D * g:D * g + D], hT[:, s, R * g:R * g + R], w["wqkv"][:, 2 * D:3 * D], start=True, stop=True)
                    last.then_inc(qkv_ps, 1)
                for p in pair:
                    s = p % 2
                    done(pe, qk_sb, p)
                    for g in range(PG):
                        for i in range(2):
                            last = nc.tensor.transpose(ps[:, s, 2, 2 * R * g + R * i:2 * R * g + R * i + R],
                                                       qk[:, s, g, i].rearrange("p h t i -> p (h t i)"), ident[:])
                    last.then_inc(qkT_ps, 1)
                    done(pe, v_sb, p)
                    for b in range(4):
                        last = mm(ps[:, s, b // 2, 256 * (b % 2):256 * (b % 2) + 256], w["place"][:, b, :],
                                  v[:, s].rearrange("p g d -> p (g d)"), start=True, stop=True)
                    last.then_inc(va_ps, 1)
                for p in pair:
                    s = p % 2
                    done(pe, va_sb, p)
                    for b in range(4, 8):
                        last = mm(ps[:, s, b // 2 - 2, 256 * (b % 2):256 * (b % 2) + 256], w["place"][:, b, :],
                                  v[:, s].rearrange("p g d -> p (g d)"), start=True, stop=True)
                    last.then_inc(vb_ps, 1)
                for p in pair:
                    s = p % 2
                    done(pe, km_sb, p)
                    done(pe, ka_sb, p)
                    done(pe, kp_sb, p)
                    for g in range(PG):
                        for b in TURNS:
                            rows = slice(b // 2 * 32, b // 2 * 32 + 32)
                            last = mm(ps[rows, s, 3, 256 * g:256 * g + 256], qM[:, s, g, R * b + rows.start:R * b + rows.stop],
                                      kM[:, s, g, b].rearrange("p h k -> p (h k)"), start=b % 2 == 0, stop=b % 2 == 1)
                    last.then_inc(s_ps, 1)
                for p in pair:
                    s = p % 2
                    done(pe, pn_sb, p)
                    for g in range(PG):
                        for i in range(2):
                            last = nc.tensor.transpose(ps[:, s, 2, 2 * R * g + R * i:2 * R * g + R * i + R],
                                                       sm[:, s, g, 8 * i:8 * i + 8].rearrange("p h k -> p (h k)"), ident[:])
                    last.then_inc(pT_ps, 1)
                for p in pair:
                    s = p % 2
                    done(pe, PT_sb, p)
                    done(pe, vb_sb, p)
                    for g in range(PG):
                        for b in range(NB):
                            for i in range(2):
                                last = mm(ps[64 * i:64 * i + 64, s, 3, R * g + K16 * b:R * g + K16 * b + K16],
                                          VM[:, s, b, g, 64 * i:64 * i + 64], PT[:, s, g, i, K16 * b:K16 * b + K16], start=True, stop=True)
                    last.then_inc(o_ps, 1)
                for p in pair:
                    s = p % 2
                    done(pe, oT_sb, p)
                    for g in range(PG):
                        last = mm(ps[:, s, 2, D * g:D * g + D], oT[:, s, g, :], w["wo"][:], start=True, stop=True)
                    last.then_inc(y_ps, 1)
                for p in pair:
                    s = p % 2
                    done(pe, hn2_sb, p)
                    for g in range(PG):
                        last = nc.tensor.transpose(ps[:, s, 3, R * g:R * g + R], hn[:, s, g, :], ident[:])
                    last.then_inc(ht2_ps, 1)
                for p in pair:
                    s = p % 2
                    done(pe, ht2_sb, p)
                    for c in range(FF // 128):
                        last = mm(ps[:, s, c // 2, 256 * (c % 2):256 * (c % 2) + 256], w["w1"][:, 128 * c:128 * c + 128], hT[:, s], start=True, stop=True)
                        if c % 2 == 1:
                            last.then_inc(h1_ps, 1)
                for p in pair:
                    s = p % 2
                    done(pe, gT_sb, p, 2)
                    for g in range(PG):
                        for c in range(FF // 128):
                            last = mm(ps[:, s, 2, D * g:D * g + D], gT[:, s, c, R * g:R * g + R], w["w2"][:, c, :], start=c == 0, stop=c == FF // 128 - 1)
                    last.then_inc(h2_ps, 1)
                for p in pair:
                    s = p % 2
                    done(pe, pm_sb, p)
                    for g in range(PG):
                        for i in range(2):
                            last = mm(ps[:, s, 2 * g + i, :], GT[:, s, g, :], VM[:, s, 4 * i:4 * i + 4, g, :], start=True, stop=True)
                    last.then_inc(sc_ps, 1)


def store_normed(nc, st, out):
    with ExitStack() as ctx:
        f = Frame(nc, ctx, "store")
        PARTS = 8
        step = B // PARTS
        (low, high, gone) = f.sems("low", "high", "gone")
        block = f.block()
        dst = out.rearrange("b s d -> s b d")

        @block.vector
        def _(dve):
            for i in range(PARTS):
                for b in range(step * i, step * i + step // 2):
                    nc.vector.tensor_scalar(st.X[:, b, :], st.X[:, b, :], st.MEAN[:, b:b + 1], st.RSTD[:, b:b + 1],
                                            ALU.subtract, ALU.mult).then_inc(low, 1)

        @block.scalar
        def _(act):
            for i in range(PARTS):
                for b in range(step * i + step // 2, step * i + step):
                    nc.scalar.activation(st.X[:, b, :], st.X[:, b, :], ACT.Identity, scale=st.RSTD[:, b:b + 1],
                                         bias=st.SHIFT[:, b:b + 1]).then_inc(high, 1)

        @block.sync
        def _(sp):
            for i in range(PARTS):
                sp.wait_ge(low, step // 2 * (i + 1))
                sp.wait_ge(high, step // 2 * (i + 1))
                sp.dma_start(dst[:, step * i:step * i + step, :], st.X[:, step * i:step * i + step, :]).then_inc(gone, 16)
            sp.wait_ge(gone, 16 * PARTS)



def rows(a):
    return np.ascontiguousarray(a)


def block_diagonal(n, width, dtype=np.float32):
    i = np.arange(n) // width
    return (i[:, None] == i[None, :]).astype(dtype)


def layouts(a):
    out = {"x": a["x"], "ctx": a["ctx_1024"], "kmask": a["mask_Bx1xSxS2_ik1"].reshape(B, S, SC)}
    out["ident"] = np.eye(128, dtype=np.float32)
    out["bd8"] = block_diagonal(128, HD)
    wq = a["L0_attn_q_weight"].reshape(D, D)
    wv = a["L0_attn_v_weight"].reshape(D, D)
    zero = np.zeros((D, 32), np.float32)
    out["a_wq"], out["a_wqT"], out["a_wv"] = rows(wq), rows(wq.T), rows(wv)
    out["a_wq3"] = np.stack([np.concatenate([wq[:, 32 * g:32 * g + 32]] * 3 + [zero], axis=1) for g in range(4)], 1)
    mask = np.zeros((128, 4), np.float32)
    for row in range(96):
        mask[row, row % 32 // HD] = 1.0 if row < 32 else -0.5
    out["a_mask"] = mask
    ow = a["L0_attn_out_w"].T.reshape(8, 2, HD, D)
    outw = np.zeros((2, 64, 2, 2, D), np.float32)
    for j in range(2):
        outw[j, :, j] = ow.transpose(0, 2, 1, 3).reshape(64, 2, D)
    out["a_outw"] = outw.reshape(128, 2, 2, D)
    out["a_outb"] = a["L0_attn_out_b"].reshape(1, D)
    for name in ("Wq", "Wk", "Wv"):
        out["b_" + name.lower()] = np.tile(a["L0_xattn_" + name], (H, H))
    out["b_woT"], out["b_bo"] = rows(a["L0_xattn_Wo"].T), a["L0_xattn_bo"].reshape(1, D)
    out["b_head"] = rows(block_diagonal(D, HD)[:, ::HD])
    out["b_sel"] = rows(block_diagonal(D, HD)[::HD])
    for k, shared in (("1", "L0_ffn_sh_w1"), ("3", "L0_ffn_sh_w3")):
        out["c_w" + k] = rows(np.concatenate([a["L0_ffn_exp_w" + k].transpose(1, 0, 2), a[shared].reshape(D, 2, D)], axis=1))
    out["c_w2"] = rows(np.concatenate([a["L0_ffn_exp_w2"], a["L0_ffn_sh_w2"].reshape(2, D, D)]).transpose(1, 0, 2))
    for name in ("lin0", "lin1"):
        out["c_" + name], out[f"c_{name}b"] = a[f"L0_ffn_{name}_w"], a[f"L0_ffn_{name}_b"].reshape(D, 1)
    for s in "12":
        for w in "12":
            out[f"c_s{s}w{w}"], out[f"c_s{s}b{w}"] = a[f"L0_ffn_swi{s}_w{w}"], a[f"L0_ffn_swi{s}_b{w}"].reshape(D, 1)
    out["c_gate"] = rows(a["L0_ffn_gate_w"].T)
    out["c_iota"] = np.tile(np.arange(E, dtype=np.float32), (128, TOPK))
    for name in ("Wq", "Wk"):
        out[f"e_{name.lower()}T"] = rows(a["L1_xattn_" + name].reshape(D, H, DK).transpose(2, 1, 0))
    out["e_wv"] = a["L1_xattn_Wv"]
    out["e_wo"] = rows(a["L1_xattn_Wo"].reshape(H // 2, 2 * DK, D).transpose(1, 0, 2))
    out["d_wqkv"] = np.concatenate([a["L1_attn_Wq"].T, a["L1_attn_Wk"].T, a["L1_attn_Wv"].T], axis=1)
    out["d_bqkv"] = np.concatenate([a["L1_attn_bq"], a["L1_attn_bk"], a["L1_attn_bv"]]).reshape(1, 3 * D)
    out["d_bd"] = np.concatenate([block_diagonal(D, HD), block_diagonal(D, HD)[:, ::HD]], axis=1)
    out["d_wo"], out["d_bo"] = rows(a["L1_attn_Wo"].T), a["L1_attn_bo"].reshape(1, D)
    picked = np.minimum(np.arange(4), a["L1_ffn_position_ids"].shape[0] - 1)
    out["f_pos"] = rows(a["L1_ffn_position_ids"][picked, :S].T)
    out["f_amask"] = rows(a["L1_ffn_attention_mask"][:, 0, :S, :S].transpose(1, 0, 2))
    out["f_inv"] = (np.float32(1.0) / np.float32(10000.0) ** (np.arange(0, HD, 2, dtype=np.float32) / np.float32(HD))).reshape(1, 4)
    out["f_token"] = np.arange(S, dtype=np.float32).reshape(S, 1)
    out["f_router"], out["f_routerb"] = rows(a["L1_ffn_router_w"].T), a["L1_ffn_router_b"].reshape(1, 1)
    out["f_wqkv"] = np.concatenate([a["L1_ffn_wq"], a["L1_ffn_wk"], a["L1_ffn_wv"]], axis=1)
    out["f_wo"], out["f_w1"] = a["L1_ffn_wo"], a["L1_ffn_w1"]
    out["f_w2"] = rows(a["L1_ffn_w2"].reshape(4, 128, D).transpose(1, 0, 2))
    out["f_ln1"], out["f_ln2"] = a["L1_ffn_ln1"].reshape(D, 1), a["L1_ffn_ln2"].reshape(D, 1)
    row = np.arange(128)
    own = np.zeros((128, 8), np.float32)
    own[row, row // 16] = 1.0
    kind = np.zeros((128, 8, 4), np.float32)
    for g in range(8):
        kind[row, g, np.minimum(8 * g + row // 16, 3)] = 1.0
    place = np.zeros((128, 8, 128), np.float32)
    for b in range(8):
        for i in range(8):
            place[16 * b + np.arange(16), b, 16 * i + np.arange(16)] = 1.0
    out["f_own"], out["f_kind"], out["f_place"] = own, kind, place
    out["f_vown"] = np.repeat(own, HD, axis=1)
    out["f_head"] = rows(block_diagonal(D, HD)[:, ::HD])
    return out


SPREAD = ("f_inv", "f_router", "f_routerb", "a_outb", "b_bo", "d_bqkv", "d_bo")


class Stream:

    def __init__(self, nc, ctx):
        def sb(name, shape):
            return ctx.enter_context(nc.sbuf_tensor(name, shape, F32))
        self.X = sb("X", [S, B, D])
        self.STATS = sb("STATS", [S, B, 6])
        self.MEAN, self.RSTD = sb("MEAN", [S, B]), sb("RSTD", [S, B])
        self.SHIFT = sb("SHIFT", [S, B])
        self.ident = sb("identity", [128, 128])
        self.w = {}


def constants(nc, ctx, st, dram):
    first, later = [(st.ident[:], dram["ident"])], []
    for name, ap in dram.items():
        if name in ("x", "ctx", "kmask", "scratch", "ident") or name.startswith("f_"):
            continue
        shape, src = list(ap.shape), ap
        if name in SPREAD:
            shape[0] = 128
            src = ap.broadcast_to(shape)
        t = st.w[name] = ctx.enter_context(nc.sbuf_tensor("w_" + name, shape, ap.dtype))
        (first if name[:2] == "a_" or name == "bd8" else later).append((t[:], src))
    st.CTX = ctx.enter_context(nc.sbuf_tensor("CTX", [SC, B, D], F32))
    later.append((st.CTX[:], dram["ctx"].rearrange("b k d -> k b d")))
    load(nc, first)
    return later



def build(nc, dram, out, sums):
    with ExitStack() as ctx:
        st = Stream(nc, ctx)
        with ExitStack() as held:
            later = constants(nc, held, st, dram)
            phase_a(nc, st, dram["x"], sums, later)
            row_stats(nc, st)
            for name, phase in (("b", phase_b), ("c", phase_c), ("d", phase_d), ("e", phase_e)):
                norm_rows(nc, st, "norm_" + name)
                phase(nc, st, dram)
        norm_rows(nc, st, "norm_f")
        phase_f(nc, st, dram)
        norm_rows(nc, st, "norm_out")
        store_normed(nc, st, out)


def kernel(**inputs):
    import concourse.bacc as bacc
    from concourse.bass_utils import run_bass_kernel_spmd

    nc = bacc.Bacc("TRN2", target_bir_lowering=False, num_devices=1)
    arrays, dram = {}, {}
    for name, a in layouts(inputs).items():
        arrays[name + "_dram"] = np.ascontiguousarray(a)
        dram[name] = nc.dram_tensor(name + "_dram", a.shape, mybir.dt.from_np(a.dtype), kind="ExternalInput").ap()
    out = nc.dram_tensor("out_dram", (B, S, D), F32, kind="ExternalOutput").ap()
    sums = nc.dram_tensor("sums_dram", (B, S, D), F32, kind="Internal").ap()
    dram["scratch"] = nc.dram_tensor("scratch_dram", (B, 2 * K16), F32, kind="Internal").ap()
    build(nc, dram, out, sums)
    r = run_bass_kernel_spmd(nc, [arrays], core_ids=[0])
    return r.results[0]["out_dram"]
```
